# Optimizing a Trainium2 kernel written in Bass

```python
import numpy as np
import jax
import jax.numpy as jnp

def _softmax(x, axis=-1):
    return jax.nn.softmax(x, axis=axis)

def _gelu(x):
    return jax.nn.gelu(x, approximate=True)

def _silu(x):
    return jax.nn.silu(x)

def _sigmoid(x):
    return jax.nn.sigmoid(x)

def _layernorm(x, axis=-1, eps=1e-05):
    m = jnp.mean(x, axis=axis, keepdims=True)
    v = jnp.var(x, axis=axis, keepdims=True)
    return (x - m) / jnp.sqrt(v + eps)

def _scatter_add(tgt, idx, src, axis=0):
    return tgt.at[idx].add(src)

def _segment_sum(src, seg, n):
    return jax.ops.segment_sum(src, seg, n)
kernel_name = 'mk_xattn_ffn_d1_seqx_r4_4d56be'

def setup_inputs(seed: int=0):
    np.random.seed(seed)
    _w = jnp.asarray

    def _rec_inputs():
        import jax
        import jax.numpy as jnp
        _rk = jax.random.key(seed)
        x = 7.22e-05 + 1 * jax.random.normal(jax.random.fold_in(_rk, 1), (16, 256, 256), jnp.float32)
        _lenS = 256 - jax.random.randint(jax.random.fold_in(_rk, 7), (16,), 0, max(1, 256 // 4) + 1, jnp.int32)
        _lenS2 = 256 - jax.random.randint(jax.random.fold_in(_rk, 8), (16,), 0, max(1, 256 // 4) + 1, jnp.int32)
        _ctx_1024P = jax.random.normal(jax.random.fold_in(_rk, 11), (16, 16, 256), jnp.float32)
        _ctx_1024c = jax.random.dirichlet(jax.random.fold_in(_rk, 511), 0.3 * jnp.ones((16,), jnp.float32), (16, 256))
        _ctx_1024t = jnp.einsum('bsk,bkd->bsd', _ctx_1024c, _ctx_1024P)
        _ctx_1024t = _ctx_1024t * jax.lax.rsqrt(jnp.mean(jnp.square(_ctx_1024t)) + 1e-12) * 0.953939
        ctx_1024 = 4.13588e-05 + 0.999923 * (_ctx_1024t + 0.3 * jax.random.normal(jax.random.fold_in(_rk, 611), (16, 256, 256), jnp.float32))
        itok_BxS2_0_2047 = jax.random.randint(jax.random.fold_in(_rk, 12), (16, 256), 0, 512, jnp.int32)
        return (x, ctx_1024, itok_BxS2_0_2047)
    x, ctx_1024, itok_BxS2_0_2047 = _rec_inputs()

    def _L0_xattn_setup():
        import jax, jax.numpy as jnp
        import numpy as np
        DIM = 256
        HEADS = 16
        HEAD_DIM = DIM // HEADS
        SCALE = HEAD_DIM ** (-0.5)
        key = jax.random.key(seed)
        ks = jax.random.split(key, 13)
        B, Nq, Nk = (4, 512, 512)
        s = DIM ** (-0.5)
        return {'query': jax.random.normal(ks[0], (B, Nq, DIM), jnp.float32), 'key': jax.random.normal(ks[1], (B, Nk, DIM), jnp.float32), 'value': jax.random.normal(ks[2], (B, Nk, DIM), jnp.float32), 'qpos': jax.random.randint(ks[3], (B, Nq), 0, Nq), 'kpos': jax.random.randint(ks[4], (B, Nk), 0, Nk), 'Wq': jax.random.normal(ks[5], (DIM, DIM), jnp.float32) * s, 'bq': jnp.zeros((DIM,), jnp.float32), 'Wk': jax.random.normal(ks[6], (DIM, DIM), jnp.float32) * s, 'bk': jnp.zeros((DIM,), jnp.float32), 'Wv': jax.random.normal(ks[7], (DIM, DIM), jnp.float32) * s, 'bv': jnp.zeros((DIM,), jnp.float32), 'Wo': jax.random.normal(ks[8], (DIM, DIM), jnp.float32) * s, 'bo': jnp.zeros((DIM,), jnp.float32)}
    _L0_xattn_all = _L0_xattn_setup()
    _L0_xattn_in = {k: v for k, v in _L0_xattn_all.items() if k in ('Wq', 'bq', 'Wk', 'bk', 'Wv', 'bv', 'Wo', 'bo')}
    del _L0_xattn_all

    def _L0_ffn_setup():
        import jax, jax.numpy as jnp
        import numpy as np
        TOP_K = 2
        EPS = 1e-09
        key = jax.random.key(seed)
        ks = jax.random.split(key, 6)
        B, T, D, H, E = (4, 512, 256, 512, 8)
        x = jax.random.normal(ks[0], (B, T, D), dtype=jnp.float32)
        Wg = jax.random.normal(ks[1], (E, D), dtype=jnp.float32) * 0.02
        W1 = jax.random.normal(ks[2], (E, 2 * H, D), dtype=jnp.float32) * 0.02
        b1 = jax.random.normal(ks[3], (E, 2 * H), dtype=jnp.float32) * 0.02
        Wo = jax.random.normal(ks[4], (D, H), dtype=jnp.float32) * 0.02
        bo = jax.random.normal(ks[5], (D,), dtype=jnp.float32) * 0.02
        return {'x': x, 'Wg': Wg, 'W1': W1, 'b1': b1, 'Wo': Wo, 'bo': bo}
    _L0_ffn_all = _L0_ffn_setup()
    _L0_ffn_in = {k: v for k, v in _L0_ffn_all.items() if k in ('Wg', 'W1', 'b1', 'Wo', 'bo')}
    del _L0_ffn_all
    return {'x': x, 'ctx_1024': ctx_1024, 'itok_BxS2_0_2047': itok_BxS2_0_2047, 'L0_xattn_Wq': _L0_xattn_in['Wq'], 'L0_xattn_bq': _L0_xattn_in['bq'], 'L0_xattn_Wk': _L0_xattn_in['Wk'], 'L0_xattn_bk': _L0_xattn_in['bk'], 'L0_xattn_Wv': _L0_xattn_in['Wv'], 'L0_xattn_bv': _L0_xattn_in['bv'], 'L0_xattn_Wo': _L0_xattn_in['Wo'], 'L0_xattn_bo': _L0_xattn_in['bo'], 'L0_ffn_Wg': _L0_ffn_in['Wg'], 'L0_ffn_W1': _L0_ffn_in['W1'], 'L0_ffn_b1': _L0_ffn_in['b1'], 'L0_ffn_Wo': _L0_ffn_in['Wo'], 'L0_ffn_bo': _L0_ffn_in['bo']}

def reference(x, ctx_1024, itok_BxS2_0_2047, L0_xattn_Wq, L0_xattn_bq, L0_xattn_Wk, L0_xattn_bk, L0_xattn_Wv, L0_xattn_bv, L0_xattn_Wo, L0_xattn_bo, L0_ffn_Wg, L0_ffn_W1, L0_ffn_b1, L0_ffn_Wo, L0_ffn_bo):
    import jax
    import jax.numpy as jnp

    def _L0_xattn_ref(query, key, value, qpos, kpos, Wq, bq, Wk, bk, Wv, bv, Wo, bo):
        import jax, jax.numpy as jnp
        import numpy as np
        DIM = 256
        HEADS = 16
        HEAD_DIM = DIM // HEADS
        SCALE = HEAD_DIM ** (-0.5)
        B, Nq, C = query.shape

        def split_heads(x):
            return x.reshape(x.shape[0], x.shape[1], HEADS, HEAD_DIM).transpose(0, 2, 1, 3)
        q = split_heads(query @ Wq + bq)
        k = split_heads(key @ Wk + bk)
        v = split_heads(value @ Wv + bv)
        attn = jnp.einsum('bhqd,bhkd->bhqk', q, k) * SCALE
        attn = jax.nn.softmax(attn, axis=-1)
        x = jnp.einsum('bhqk,bhkd->bhqd', attn, v)
        x = x.transpose(0, 2, 1, 3).reshape(B, Nq, C)
        return x @ Wo + bo

    def _L0_ffn_ref(x, Wg, W1, b1, Wo, bo):
        import jax, jax.numpy as jnp
        import numpy as np
        TOP_K = 2
        EPS = 1e-09
        E = Wg.shape[0]
        gate_logits = jnp.einsum('btd,ed->bte', x, Wg)
        gate_scores = jax.nn.softmax(gate_logits, axis=-1)
        topk_val, topk_idx = jax.lax.top_k(gate_scores, TOP_K)
        topk_val = topk_val / (topk_val.sum(axis=-1, keepdims=True) + EPS)
        comb = (jax.nn.one_hot(topk_idx, E, dtype=x.dtype) * topk_val[..., None]).sum(axis=-2)
        out = jnp.zeros_like(x)
        for e in range(E):
            h = jnp.einsum('btd,hd->bth', x, W1[e]) + b1[e]
            a, b = jnp.split(h, 2, axis=-1)
            g = a * jax.nn.sigmoid(b)
            eo = jnp.einsum('bth,dh->btd', g, Wo) + bo
            out = out + eo * comb[..., e:e + 1]
        return out
    x = x + _L0_xattn_ref(_layernorm(x, axis=-1), ctx_1024, ctx_1024, itok_BxS2_0_2047, itok_BxS2_0_2047, L0_xattn_Wq, L0_xattn_bq, L0_xattn_Wk, L0_xattn_bk, L0_xattn_Wv, L0_xattn_bv, L0_xattn_Wo, L0_xattn_bo)
    x = x + _L0_ffn_ref(_layernorm(x, axis=-1), L0_ffn_Wg, L0_ffn_W1, L0_ffn_b1, L0_ffn_Wo, L0_ffn_bo)
    return x

_drawn_inputs = setup_inputs


def setup_inputs(seed=0):
    import zlib

    import numpy as np

    out = dict(_drawn_inputs(seed))
    spreads = {'L0_xattn_bq': (0.0, 0.377),
     'L0_xattn_bk': (0.0, 0.8),
     'L0_xattn_bv': (0.0, 0.1),
     'L0_xattn_bo': (0.0, 0.1)}
    factors = {'L0_ffn_b1': 8.0, 'L0_ffn_bo': 3.11}
    for name, (base, spread) in spreads.items():
        noise = np.random.default_rng([zlib.crc32(name.encode()), seed]).standard_normal(out[name].shape)
        drawn = base * np.exp(spread * noise) if base else spread * noise
        out[name] = jnp.asarray(drawn.astype(out[name].dtype))
    for name, factor in factors.items():
        out[name] = (out[name] * factor).astype(out[name].dtype)
    return out
```

```python
from contextlib import ExitStack

import concourse.bass as bass
import numpy as np
from concourse import mybir

F32 = mybir.dt.float32
F32R = mybir.dt.float32r
BF16 = mybir.dt.bfloat16
I32 = mybir.dt.int32
U32 = mybir.dt.uint32
ALU = mybir.AluOpType
ACT = mybir.ActivationFunctionType
AX = mybir.AxisListType

P = 128
BATCH = 16
TOK = 256
D = 256
HEADS = 16
HD = D // HEADS
KC = D // P
QT = TOK // P
QUAD = 4
NQ = HEADS // QUAD
NT = BATCH * QT
TOKENS = BATCH * TOK
EXPERTS = 8
HID = 512
ROW = D + EXPERTS
SLOT_TILES = (2 * TOKENS + EXPERTS * (P - 1)) // P
EPS = 1e-5
TOP_EPS = 1e-9
MAGIC = 1597463007.0
NEWTON_STEPS = 3
M_ROW = 3 * HD


def at_least(eng, sem, tile, per_tile, nth):
    if isinstance(tile, int) and tile < 0:
        return
    eng.wait_ge(sem, tile * per_tile + nth)


def attention_program(nc, io, keep, ctx):
    def sb(name, shape, dt=F32):
        return ctx.enter_context(nc.sbuf_tensor(name, shape, dt))

    def sem(name):
        return ctx.enter_context(nc.semaphore(name))

    ident = keep["ident"]
    w_raw = sb("w_raw", [P, 4, KC, D])
    w_hi = sb("w_hi", [P, 4, KC, D], F32R)
    w_lo = sb("w_lo", [P, 4, KC, D], F32R)
    WQ, WK, WV, WO = range(4)
    wg = sb("wg", [P, KC, EXPERTS])
    bqk = sb("bqk", [P, 2, KC])
    bv_all = sb("bv_all", [P, D])
    bo_all = sb("bo_all", [P, D])
    zeros = sb("zeros", [HEADS, TOK])
    ones = sb("ones", [HEADS, TOK])
    x_rows = sb("x_rows", [P, QT, D])
    ctx_rows = sb("ctx_rows", [P, QT, D])
    xn = sb("xn", [P, QT, D])
    ctxT_hi = sb("ctxT_hi", [P, KC, TOK], F32R)
    ctxT_lo = sb("ctxT_lo", [P, KC, TOK], F32R)
    xT_hi = sb("xT_hi", [P, KC, TOK], F32R)
    xT_lo = sb("xT_lo", [P, KC, TOK], F32R)
    q_hi = sb("q_hi", [P, KC, TOK], F32R)
    q_lo = sb("q_lo", [P, KC, TOK], F32R)
    k_hi = sb("k_hi", [P, KC, TOK], F32R)
    k_lo = sb("k_lo", [P, KC, TOK], F32R)
    qs = [sb(f"q_stack{p}", [P, HEADS, TOK], F32R) for p in range(2)]
    ks = [sb(f"k_stack{p}", [P, HEADS, TOK], F32R) for p in range(2)]
    vals = [sb(f"values{p}", [P, QT, HEADS, 2 * HD]) for p in range(2)]
    neg_max = sb("neg_max", [P, QT, HEADS])
    m_row = sb("m_row", [QUAD, NQ, TOK], F32R)
    probs = sb("probs", [P, 8, QT * TOK])
    quad_sb = sb("quad_sb", [P, NQ, TOK])
    recip = sb("recip", [P, QT, HEADS])
    attn = sb("attn", [P, QT, D])
    attnT_hi = sb("attnT_hi", [P, KC, TOK], F32R)
    attnT_lo = sb("attnT_lo", [P, KC, TOK], F32R)
    x_again = sb("x_again", [P, QT, D])
    x_res = sb("x_res", [P, QT, D])
    x2 = sb("x2", [P, QT, D])
    xn2 = sb("xn2", [P, QT, D])
    xn2T = sb("xn2T", [P, KC, TOK])
    eps = sb("eps", [P, QT])
    stats1 = sb("stats1", [P, QT, 6])
    stats2 = sb("stats2", [P, QT, 6])
    mv1 = sb("mv1", [P, QT, 2])
    mv2 = sb("mv2", [P, QT, 2])
    norm1 = sb("norm1", [P, 4, QT])
    norm2 = sb("norm2", [P, 4, QT])
    logits = keep["logits"]

    st = ctx.enter_context(nc.psum_tensor("scoresT", [P, 2, QT * TOK], F32))
    mx = ctx.enter_context(nc.psum_tensor("scores", [P, 2, QT * TOK], F32))
    ov = ctx.enter_context(nc.psum_tensor("quad_out", [P, 2, 512], F32))
    misc = ctx.enter_context(nc.psum_tensor("misc", [P, 2, 512], F32))

    s = {n: sem("a_" + n) for n in (
        "weights_in w_hi_done w_lo_done bias_done cleared values_cleared ones_set ones_placed "
        "x_in ctx_in x_again_in k_stacked q_stacked m_placed x2_stored xn2_stored "
        "ctxT_filled xT_filled k_filled q_filled v_filled mT_filled scores_filled scoresT_filled "
        "pv_filled oT_filled attnT_filled proj_filled xn2T_filled gate_filled "
        "ctxT_hi_done xT_hi_done k_hi_done q_hi_done exp_done quad_saved attnT_hi_done xn2T_saved "
        "ctxT_lo_done xT_lo_done k_lo_done q_lo_done v_saved m_row_done max_done recip_done "
        "attn_done attnT_lo_done x2_done ln1_stats ln2_stats gate_saved "
        "xn_done x_res_done xn2_done").split()}
    K_DMAS, Q_DMAS = 6 * 16, 7 * 16

    x_dram = io["x"].rearrange("b (t p) d -> b p t d", p=P)
    ctx_dram = io["ctx"].rearrange("b (t p) d -> b p t d", p=P)
    out_dram = io["out"][0:TOKENS, :].rearrange("(b t p) d -> b p t d", p=P, t=QT)
    xn2_dram = io["rows"][:, 0:D].rearrange("(b t p) d -> b p t d", p=P, t=QT)

    def active(b):
        return not isinstance(b, int) or 0 <= b < BATCH

    def at_least(eng, sem, b, per_row, nth):
        if active(b):
            eng.wait_ge(sem, b * per_row + nth)

    FILLS = [("ctxT", 1), ("m3", -1), ("xT", 1), ("xn2T", -2), ("k", 1), ("m0", 0), ("q", 1),
             ("gate", -2), ("m1", 0), ("v", 1), ("oT0", -1), ("oT1", -1), ("m2", 0),
             ("attnT", -1), ("proj", -1)]
    ORDER = {name: n for n, (name, _) in enumerate(FILLS)}
    def bank(par, name):
        return misc[:, (par + ORDER[name]) % 2, :]

    def run(eng, iteration):
        for i in range(-1, 4):
            iteration(i, i % 2)
        with eng.Fori(2, 7) as pair:
            iteration(pair * 2, 0)
            iteration(pair * 2 + 1, 1)
        for i in (14, 15, 16, 17):
            iteration(i, i % 2)

    block = ctx.enter_context(nc.Block())

    @block.sync
    def _(sp):
        for n, w in enumerate(("Wq", "Wk", "Wv", "Wo")):
            sp.dma_start(w_raw[:, n], io[w].rearrange("(c p) n -> p c n", p=P)).then_inc(s["weights_in"], 16)
        sp.dma_start(wg[:], io["WgT"].rearrange("(c p) n -> p c n", p=P)).then_inc(s["weights_in"], 16)
        for n, b in enumerate(("bq", "bk")):
            sp.dma_start(bqk[:, n], io[b].rearrange("(c p) -> p c", p=P),
                         allow_slow_non_contiguous=True).then_inc(s["weights_in"], 16)
        sp.dma_start(bv_all[:], io["bv"].partition_broadcast(P)).then_inc(s["weights_in"], 16)
        sp.dma_start(bo_all[:], io["bo"].partition_broadcast(P)).then_inc(s["weights_in"], 16)
        sp.dma_start(ident[:], io["ident"]).then_inc(s["weights_in"], 16)
        sp.wait_ge(s["ones_set"], 1)
        sp.wait_ge(s["cleared"], 4)
        for p in range(2):
            sp.dma_start(ks[p][M_ROW:M_ROW + 1].bitcast(F32), ones[:]).then_inc(s["ones_placed"], 16)

        def stack(b, par, name, natural_hi, natural_lo, dst, order):
            for part, which in enumerate(order):
                for c in range(KC):
                    src = (natural_hi, natural_lo)[which][:, c, :]
                    to = dst[par][part * HD:(part + 1) * HD, c * 8:(c + 1) * 8, :]
                    sp.dma_start(to.bitcast(F32), src.bitcast(F32)).then_inc(s[name], 16)

        def place_m(i, par, lag, g):
            b = i + lag
            at_least(sp, s["m_row_done"], b, NQ, g + 1)
            sp.dma_start(qs[(par + lag) % 2][M_ROW:M_ROW + 1, QUAD * g:QUAD * (g + 1), :].bitcast(F32),
                         m_row[:, g, :].bitcast(F32)).then_inc(s["m_placed"], 16)

        def iteration(i, par):
            if active(i + 2):
                at_least(sp, s["xn_done"], i + 1, 1, 1)
                sp.dma_start(x_rows[:], x_dram[i + 2]).then_inc(s["x_in"], 16)
            if active(i - 1):
                place_m(i, par, -1, 3)
            if active(i - 2):
                at_least(sp, s["x2_done"], i - 2, 1, 1)
                sp.dma_start(out_dram[i - 2], x2[:]).then_inc(s["x2_stored"], 16)
            if active(i + 2):
                at_least(sp, s["ctxT_filled"], i + 1, 1, 1)
                sp.dma_start(ctx_rows[:], ctx_dram[i + 2]).then_inc(s["ctx_in"], 16)
            if active(i - 1):
                at_least(sp, s["x_res_done"], i - 2, 1, 1)
                sp.dma_start(x_again[:], x_dram[i - 1]).then_inc(s["x_again_in"], 16)
            if active(i - 2):
                at_least(sp, s["xn2_done"], i - 2, 1, 1)
                sp.dma_start(xn2_dram[i - 2], xn2[:]).then_inc(s["xn2_stored"], 16)
            if active(i):
                place_m(i, par, 0, 0)
            if active(i + 1):
                nxt = (par + 1) % 2
                at_least(sp, s["scoresT_filled"], i - 1, HEADS, HEADS)
                at_least(sp, s["k_lo_done"], i + 1, 1, 1)
                stack(i + 1, nxt, "k_stacked", k_hi, k_lo, ks, (0, 1, 0))
                at_least(sp, s["q_lo_done"], i + 1, 1, 1)
                stack(i + 1, nxt, "q_stacked", q_hi, q_lo, qs, (0, 0, 1))
                sp.dma_start(qs[nxt][M_ROW:M_ROW + 1].bitcast(F32), zeros[:]).then_inc(s["q_stacked"], 16)
            if active(i):
                place_m(i, par, 0, 1)
                place_m(i, par, 0, 2)

        sp.dma_start(x_rows[:], x_dram[0]).then_inc(s["x_in"], 16)
        sp.dma_start(ctx_rows[:], ctx_dram[0]).then_inc(s["ctx_in"], 16)
        run(sp, iteration)
        sp.wait_ge(s["x2_stored"], 16 * BATCH)
        sp.wait_ge(s["xn2_stored"], 16 * BATCH)

    @block.tensor
    def _(pe):
        def three(out, lhs_hi, lhs_lo, rhs_hi, rhs_lo, first, last):
            nc.tensor.matmul(out, lhs_hi, rhs_hi, start=first, stop=False)
            nc.tensor.matmul(out, lhs_hi, rhs_lo, start=False, stop=False)
            return nc.tensor.matmul(out, lhs_lo, rhs_hi, start=False, stop=last)

        def transpose_rows(rows, out):
            for c in range(KC):
                for t in range(QT):
                    last = nc.tensor.transpose(out[:, c * TOK + t * P:c * TOK + (t + 1) * P],
                                               rows[:, t, c * P:(c + 1) * P], ident[:])
            return last

        def project_T(w, src_hi, src_lo, out):
            for m in range(KC):
                for c in range(KC):
                    cols = slice(m * P, (m + 1) * P)
                    last = three(out[:, m * TOK:(m + 1) * TOK], w_hi[:, w, c, cols], w_lo[:, w, c, cols],
                                 src_hi[:, c, :], src_lo[:, c, :], c == 0, c == KC - 1)
            return last

        def project(w, src_hi, src_lo, out):
            for t in range(QT):
                for c in range(KC):
                    cols = slice(t * P, (t + 1) * P)
                    last = three(out[:, t * D:(t + 1) * D], src_hi[:, c, cols], src_lo[:, c, cols],
                                 w_hi[:, w, c, :], w_lo[:, w, c, :], c == 0, c == KC - 1)
            return last

        def fill(i, par, name):
            b = i + FILLS[ORDER[name]][1]
            if not active(b):
                return
            out = bank(par, name)
            if name == "ctxT":
                at_least(pe, s["v_saved"], i, 1, 1)
                at_least(pe, s["attnT_lo_done"], i - 2, 1, 1)
                at_least(pe, s["ctx_in"], b, 16, 16)
                transpose_rows(ctx_rows, out).then_inc(s["ctxT_filled"], 1)
            elif name == "xT":
                at_least(pe, s["ctxT_lo_done"], b, 1, 1)
                at_least(pe, s["xn_done"], b, 1, 1)
                transpose_rows(xn, out).then_inc(s["xT_filled"], 1)
            elif name == "k":
                at_least(pe, s["xT_lo_done"], b, 1, 1)
                project_T(WK, ctxT_hi, ctxT_lo, out).then_inc(s["k_filled"], 1)
            elif name == "q":
                at_least(pe, s["k_lo_done"], b, 1, 1)
                project_T(WQ, xT_hi, xT_lo, out).then_inc(s["q_filled"], 1)
            elif name == "v":
                at_least(pe, s["m_row_done"], i, NQ, 1)
                at_least(pe, s["gate_saved"], i - 2, 1, 1)
                project(WV, ctxT_hi, ctxT_lo, out).then_inc(s["v_filled"], 1)
            elif name in ("m0", "m1", "m2", "m3"):
                g = int(name[1])
                if name == "m0":
                    at_least(pe, s["q_lo_done"], i, 1, 1)
                    at_least(pe, s["m_row_done"], i - 1, NQ, 4)
                    at_least(pe, s["xn2T_saved"], i - 2, 1, 1)
                elif name == "m1":
                    at_least(pe, s["attnT_lo_done"], i - 2, 1, 1)
                    at_least(pe, s["q_lo_done"], i + 1, 1, 1)
                elif name == "m2":
                    at_least(pe, s["m_row_done"], i, NQ, 2)
                    at_least(pe, s["attn_done"], i - 1, 2, 1)
                else:
                    at_least(pe, s["m_row_done"], i - 1, NQ, 3)
                    at_least(pe, s["x2_done"], i - 2, 1, 1)
                at_least(pe, s["max_done"], b, HEADS, QUAD * (g + 1))
                for t in range(QT):
                    last = nc.tensor.transpose(out[0:QUAD, t * P:(t + 1) * P],
                                               neg_max[:, t, QUAD * g:QUAD * (g + 1)], ident[:])
                last.then_inc(s["mT_filled"], 1)
            elif name in ("oT0", "oT1"):
                t = int(name[2])
                if name == "oT0":
                    at_least(pe, s["attnT_lo_done"], i - 2, 1, 1)
                    at_least(pe, s["m_row_done"], i, NQ, 2)
                    at_least(pe, s["quad_saved"], b, NQ, NQ)
                else:
                    at_least(pe, s["gate_saved"], i - 2, 1, 1)
                    at_least(pe, s["v_saved"], i + 1, 1, 1)
                for g in range(NQ):
                    last = nc.tensor.transpose(out[:, g * P:(g + 1) * P],
                                               quad_sb[:, g, t * P:(t + 1) * P], ident[:])
                last.then_inc(s["oT_filled"], 1)
            elif name == "attnT":
                at_least(pe, s["attn_done"], b, 2, 2)
                transpose_rows(attn, out).then_inc(s["attnT_filled"], 1)
            elif name == "proj":
                at_least(pe, s["m_row_done"], i, NQ, 3)
                at_least(pe, s["attnT_lo_done"], b, 1, 1)
                project(WO, attnT_hi, attnT_lo, out).then_inc(s["proj_filled"], 1)
            elif name == "xn2T":
                at_least(pe, s["m_row_done"], i - 1, NQ, 4)
                at_least(pe, s["xn2_done"], b, 1, 1)
                transpose_rows(xn2, out).then_inc(s["xn2T_filled"], 1)
            elif name == "gate":
                at_least(pe, s["m_row_done"], i, NQ, 1)
                at_least(pe, s["xn2T_saved"], b, 1, 1)
                for t in range(QT):
                    for c in range(KC):
                        last = nc.tensor.matmul(out[:, t * EXPERTS:(t + 1) * EXPERTS],
                                                xn2T[:, c, t * P:(t + 1) * P], wg[:, c, :],
                                                start=(c == 0), stop=(c == KC - 1))
                last.then_inc(s["gate_filled"], 1)

        def scores_for_max(i, par, h):
            if h == 0:
                at_least(pe, s["k_stacked"], i, K_DMAS, K_DMAS)
                at_least(pe, s["q_stacked"], i, Q_DMAS, Q_DMAS)
            at_least(pe, s["max_done"], i if h >= 2 else i - 1, HEADS, (h - 2) % HEADS + 1)
            for t in range(QT):
                last = nc.tensor.matmul(mx[:, h % 2, t * TOK:(t + 1) * TOK], qs[par][:, h, t * P:(t + 1) * P],
                                        ks[par][:, h, :], start=True, stop=True)
            last.then_inc(s["scores_filled"], 1)

        def scores_for_exp(b, par, h):
            if h % QUAD == 0:
                at_least(pe, s["m_placed"], b, 16 * NQ, 16 * (h // QUAD + 1))
            at_least(pe, s["exp_done"], b if h >= 2 else b - 1, HEADS, (h - 2) % HEADS + 1)
            for t in range(QT):
                last = nc.tensor.matmul(st[:, h % 2, t * TOK:(t + 1) * TOK], ks[par][:, h, t * P:(t + 1) * P],
                                        qs[par][:, h, :], start=True, stop=True)
            last.then_inc(s["scoresT_filled"], 1)

        def probs_times_values(b, par, g):
            at_least(pe, s["exp_done"], b, HEADS, QUAD * (g + 1))
            at_least(pe, s["v_saved"], b, 1, 1)
            at_least(pe, s["quad_saved"], b if g >= 2 else b - 1, NQ, (g - 2) % NQ + 1)
            for t in range(QT):
                for j in range(QUAD):
                    h = QUAD * g + j
                    last = nc.tensor.matmul(ov[32 * j:32 * (j + 1), g % 2, 0:TOK], vals[par][:, t, h, :],
                                            probs[:, h % 8, t * TOK:(t + 1) * TOK],
                                            start=(t == 0), stop=(t == QT - 1),
                                            tile_position=(0, 32 * j))
            last.then_inc(s["pv_filled"], 1)

        AT_STEP = {0: ["ctxT"], 1: ["m3"], 2: ["xT"], 3: ["xn2T"], 4: ["k"], 5: ["m0"], 6: ["q"],
                   7: ["gate"], 9: ["m1"], 10: ["v"], 11: ["oT0"], 12: ["oT1"], 13: ["m2"],
                   14: ["attnT"], 15: ["proj"]}

        def iteration(i, par):
            for step in range(HEADS):
                if step < 8 and active(i - 1):
                    scores_for_exp(i - 1, (par + 1) % 2, step + 8)
                if step >= 8 and active(i):
                    scores_for_exp(i, par, step - 8)
                if step in (1, 5, 9) and active(i - 1):
                    probs_times_values(i - 1, (par + 1) % 2, (step + 3) // 4)
                if step == 13 and active(i):
                    probs_times_values(i, par, 0)
                if active(i):
                    scores_for_max(i, par, step)
                for name in AT_STEP.get(step, []):
                    fill(i, par, name)

        pe.wait_ge(s["weights_in"], 160)
        pe.wait_ge(s["w_lo_done"], 4)
        pe.wait_ge(s["cleared"], 4)
        pe.wait_ge(s["values_cleared"], 4)
        pe.wait_ge(s["ones_placed"], 32)
        run(pe, iteration)

    @block.scalar
    def _(act):
        act.wait_ge(s["weights_in"], 160)
        for n in range(4):
            nc.scalar.activation(w_hi[:, n], w_raw[:, n], ACT.Copy,
                                 scale=0.25 if n == WQ else 1.0).then_inc(s["w_hi_done"], 1)

        def hi(par, name, dst, done):
            nc.scalar.activation(dst[:].rearrange("p c t -> p (c t)"), bank(par, name),
                                 ACT.Copy).then_inc(s[done], 1)

        def biased_hi(par, name, n, dst, done):
            for c in range(KC):
                last = nc.scalar.activation(dst[:, c, :], bank(par, name)[:, c * TOK:(c + 1) * TOK],
                                            ACT.Identity, bias=bqk[:, n, c:c + 1])
            last.then_inc(s[done], 1)

        def exp(b, h):
            at_least(act, s["scoresT_filled"], b, HEADS, h + 1)
            at_least(act, s["pv_filled"], b if h >= 8 else b - 1, NQ, (h // QUAD - 2) % NQ + 1)
            nc.scalar.activation(probs[:, h % 8, :], st[:, h % 2, :], ACT.Exp).then_inc(s["exp_done"], 1)

        def save_quad(b, g):
            at_least(act, s["pv_filled"], b, NQ, g + 1)
            at_least(act, s["oT_filled"], b - 1, 2, 2)
            nc.scalar.activation(quad_sb[:, g, :], ov[:, g % 2, 0:TOK], ACT.Copy).then_inc(s["quad_saved"], 1)

        def iteration(i, par):
            for step in range(HEADS):
                if step < 8 and active(i - 1):
                    exp(i - 1, step + 8)
                if step >= 8 and active(i):
                    exp(i, step - 8)
                if step in (1, 5, 9) and active(i - 1):
                    save_quad(i - 1, (step + 3) // 4)
                if step == 13 and active(i):
                    save_quad(i, 0)
                if step == 0 and active(i + 1):
                    at_least(act, s["ctxT_filled"], i + 1, 1, 1)
                    at_least(act, s["v_filled"], i, 1, 1)
                    hi(par, "ctxT", ctxT_hi, "ctxT_hi_done")
                if step == 2 and active(i + 1):
                    at_least(act, s["xT_filled"], i + 1, 1, 1)
                    at_least(act, s["q_filled"], i, 1, 1)
                    hi(par, "xT", xT_hi, "xT_hi_done")
                if step == 3 and active(i - 2):
                    at_least(act, s["xn2T_filled"], i - 2, 1, 1)
                    at_least(act, s["gate_filled"], i - 3, 1, 1)
                    nc.scalar.activation(xn2T[:].rearrange("p c t -> p (c t)"), bank(par, "xn2T"),
                                         ACT.Copy).then_inc(s["xn2T_saved"], 1)
                if step == 4 and active(i + 1):
                    at_least(act, s["k_filled"], i + 1, 1, 1)
                    at_least(act, s["k_stacked"], i, K_DMAS, K_DMAS)
                    biased_hi(par, "k", 1, k_hi, "k_hi_done")
                if step == 6 and active(i + 1):
                    at_least(act, s["q_filled"], i + 1, 1, 1)
                    at_least(act, s["q_stacked"], i, Q_DMAS, Q_DMAS)
                    biased_hi(par, "q", 0, q_hi, "q_hi_done")
                if step == 14 and active(i - 1):
                    at_least(act, s["attnT_filled"], i - 1, 1, 1)
                    at_least(act, s["proj_filled"], i - 2, 1, 1)
                    hi(par, "attnT", attnT_hi, "attnT_hi_done")

        act.wait_ge(s["bias_done"], 1)
        run(act, iteration)

    @block.vector
    def _(dve):
        for rows in (qs[0], ks[0]):
            nc.vector.memset(rows[:].bitcast(F32), 0.0).then_inc(s["cleared"], 1)
        for p in range(2):
            nc.vector.memset(vals[p][:, :, :, HD:], 0.0).then_inc(s["values_cleared"], 1)
        dve.wait_ge(s["values_cleared"], 2)
        for p in range(2):
            nc.vector.memset(vals[p][:, :, :, HD], 1.0).then_inc(s["values_cleared"], 1)
        dve.wait_ge(s["weights_in"], 160)
        nc.vector.tensor_scalar(bqk[:, 0], bqk[:, 0], 0.25, None, ALU.mult).then_inc(s["bias_done"], 1)
        for n in range(4):
            dve.wait_ge(s["w_hi_done"], n + 1)
            nc.vector.scalar_tensor_tensor(out=w_lo[:, n], in0=w_raw[:, n], scalar=0.25 if n == WQ else 1.0,
                                           in1=w_hi[:, n].bitcast(F32), op0=ALU.mult,
                                           op1=ALU.subtract).then_inc(s["w_lo_done"], 1)
        dve.wait_ge(s["bias_done"], 1)

        def row_max(i, par, h):
            at_least(dve, s["scores_filled"], i, HEADS, h + 1)
            if h % QUAD == 0:
                at_least(dve, s["mT_filled"], i - 1, NQ, h // QUAD + 1)
            nc.vector.tensor_reduce(neg_max[:, :, h:h + 1], mx[:, h % 2, :].rearrange("p (t k) -> p t k", t=QT),
                                    AX.X, ALU.max, negate=True).then_inc(s["max_done"], 1)

        def lo(par, name, dst_hi, dst_lo, done):
            nc.vector.tensor_tensor(dst_lo[:].rearrange("p c t -> p (c t)"), bank(par, name),
                                    dst_hi[:].rearrange("p c t -> p (c t)").bitcast(F32),
                                    ALU.subtract).then_inc(s[done], 1)

        def biased_lo(par, name, n, dst_hi, dst_lo, done):
            for c in range(KC):
                last = nc.vector.scalar_tensor_tensor(
                    out=dst_lo[:, c, :], in0=bank(par, name)[:, c * TOK:(c + 1) * TOK],
                    scalar=bqk[:, n, c:c + 1], in1=dst_hi[:, c, :].bitcast(F32),
                    op0=ALU.add, op1=ALU.subtract)
            last.then_inc(s[done], 1)

        def m_to_row(i, par, lag, g):
            b = i + lag
            at_least(dve, s["mT_filled"], b, NQ, g + 1)
            at_least(dve, s["m_placed"], b - 1, 16 * NQ, 16 * NQ)
            nc.vector.tensor_copy(m_row[:, g, :], bank(par, f"m{g}")[0:QUAD, 0:TOK]).then_inc(s["m_row_done"], 1)

        def attention_rows(i, par, t):
            b = i - 1
            src = bank(par, f"oT{t}").rearrange("p (h e) -> p h e", e=32)
            at_least(dve, s["oT_filled"], b, 2, t + 1)
            at_least(dve, s["attn_done"], b - 1, 2, 2)
            nc.vector.reciprocal(recip[:, t, :].unsqueeze(2), src[:, :, HD:HD + 1]).then_inc(s["recip_done"], 1)
            at_least(dve, s["recip_done"], b, 2, t + 1)
            at_least(dve, s["attnT_filled"], b - 1, 1, 1)
            nc.vector.tensor_tensor(attn[:, t, :].rearrange("p (h e) -> p h e", e=HD), src[:, :, 0:HD],
                                    recip[:, t, :].unsqueeze(2).to_broadcast([P, HEADS, HD]),
                                    ALU.mult).then_inc(s["attn_done"], 1)

        def row_stats(rows, parts, mv, stats_done):
            for t in range(QT):
                last = nc.vector.bn_stats(parts[:, t, :], rows[:, t, :])
            dve.drain()
            for t in range(QT):
                last = nc.vector.bn_aggr(mv[:, t, :], parts[:, t, :])
            last.then_inc(s[stats_done], 1)

        def ln1_stats(b):
            at_least(dve, s["x_in"], b, 16, 16)
            at_least(dve, s["ln1_stats"], b - 1, 1, 1)
            at_least(dve, s["xn_done"], b - 1, 1, 1)
            row_stats(x_rows, stats1, mv1, "ln1_stats")

        def iteration(i, par):
            for step in range(HEADS):
                if active(i):
                    row_max(i, par, step)
                if step == 0 and active(i + 1):
                    at_least(dve, s["v_filled"], i, 1, 1)
                    at_least(dve, s["ctxT_hi_done"], i + 1, 1, 1)
                    lo(par, "ctxT", ctxT_hi, ctxT_lo, "ctxT_lo_done")
                if step == 1 and active(i - 1):
                    m_to_row(i, par, -1, 3)
                if step == 2 and active(i + 1):
                    at_least(dve, s["q_filled"], i, 1, 1)
                    at_least(dve, s["xT_hi_done"], i + 1, 1, 1)
                    lo(par, "xT", xT_hi, xT_lo, "xT_lo_done")
                if step == 4 and active(i + 1):
                    at_least(dve, s["k_stacked"], i, K_DMAS, K_DMAS)
                    at_least(dve, s["k_hi_done"], i + 1, 1, 1)
                    biased_lo(par, "k", 1, k_hi, k_lo, "k_lo_done")
                if step == 5 and active(i):
                    m_to_row(i, par, 0, 0)
                if step == 6 and active(i + 1):
                    at_least(dve, s["q_stacked"], i, Q_DMAS, Q_DMAS)
                    at_least(dve, s["q_hi_done"], i + 1, 1, 1)
                    biased_lo(par, "q", 0, q_hi, q_lo, "q_lo_done")
                if step == 7 and active(i - 2):
                    at_least(dve, s["gate_filled"], i - 2, 1, 1)
                    nc.vector.tensor_copy(logits[:, bass.ds((i - 2) * (QT * EXPERTS), QT * EXPERTS)],
                                          bank(par, "gate")[:, 0:QT * EXPERTS]).then_inc(s["gate_saved"], 1)
                if step == 8 and active(i + 2):
                    ln1_stats(i + 2)
                if step == 9 and active(i):
                    m_to_row(i, par, 0, 1)
                if step == 10 and active(i + 1):
                    at_least(dve, s["v_filled"], i + 1, 1, 1)
                    at_least(dve, s["pv_filled"], i - 1, NQ, NQ)
                    nc.vector.tensor_tensor(
                        vals[(par + 1) % 2][:, :, :, 0:HD],
                        bank(par, "v").rearrange("p (t h e) -> p t h e", t=QT, e=HD),
                        bv_all[:].rearrange("p (h e) -> p h e", e=HD).unsqueeze(1).to_broadcast([P, QT, HEADS, HD]),
                        ALU.add).then_inc(s["v_saved"], 1)
                if step in (11, 12) and active(i - 1):
                    attention_rows(i, par, step - 11)
                if step == 13 and active(i):
                    m_to_row(i, par, 0, 2)
                if step == 14 and active(i - 1):
                    at_least(dve, s["proj_filled"], i - 2, 1, 1)
                    at_least(dve, s["attnT_hi_done"], i - 1, 1, 1)
                    lo(par, "attnT", attnT_hi, attnT_lo, "attnT_lo_done")
                if step == 15 and active(i - 1):
                    b = i - 1
                    at_least(dve, s["proj_filled"], b, 1, 1)
                    at_least(dve, s["x_res_done"], b, 1, 1)
                    at_least(dve, s["x2_stored"], b - 1, 16, 16)
                    at_least(dve, s["xn2_done"], b - 1, 1, 1)
                    nc.vector.tensor_tensor(x2[:].rearrange("p t d -> p (t d)"), bank(par, "proj"),
                                            x_res[:].rearrange("p t d -> p (t d)"),
                                            ALU.add).then_inc(s["x2_done"], 1)
                    at_least(dve, s["x2_done"], b, 1, 1)
                    at_least(dve, s["ln2_stats"], b - 1, 1, 1)
                    row_stats(x2, stats2, mv2, "ln2_stats")

        ln1_stats(0)
        run(dve, iteration)

    @block.gpsimd
    def _(pool):
        nc.gpsimd.memset(ones[:], 1.0)
        nc.gpsimd.memset(eps[:], EPS)
        nc.gpsimd.memset(zeros[:], 0.0).then_inc(s["ones_set"], 1)
        for rows in (qs[1], ks[1]):
            nc.gpsimd.memset(rows[:].bitcast(F32), 0.0).then_inc(s["cleared"], 1)
        pool.wait_ge(s["weights_in"], 160)

        def normalise(rows, mv, tmp, dst, done):
            var, neg_mean, y, t = (tmp[:, n, :] for n in range(4))

            def then(_):
                pool.drain()

            then(nc.gpsimd.tensor_tensor(var, mv[:, :, 1], eps[:], ALU.add))
            then(nc.gpsimd.tensor_scalar(neg_mean, mv[:, :, 0], -1.0, None, ALU.mult))
            then(nc.gpsimd.tensor_scalar(y.bitcast(I32), var.bitcast(I32), -0.5, MAGIC, ALU.mult, ALU.add))
            for _ in range(NEWTON_STEPS):
                then(nc.gpsimd.tensor_tensor(t, y, y, ALU.mult))
                then(nc.gpsimd.tensor_tensor(t, t, var, ALU.mult))
                then(nc.gpsimd.tensor_scalar(t, t, -0.5, 1.5, ALU.mult, ALU.add))
                then(nc.gpsimd.tensor_tensor(y, y, t, ALU.mult))
            for t_ in range(QT):
                last = nc.gpsimd.tensor_scalar(dst[:, t_, :], rows[:, t_, :], neg_mean[:, t_:t_ + 1],
                                               y[:, t_:t_ + 1], ALU.add, ALU.mult)
            last.then_inc(s[done], 1)

        def first_norm(b):
            at_least(pool, s["ln1_stats"], b, 1, 1)
            at_least(pool, s["xn_done"], b - 1, 1, 1)
            at_least(pool, s["xT_filled"], b - 1, 1, 1)
            normalise(x_rows, mv1, norm1, xn, "xn_done")

        def iteration(i, par):
            if active(i - 2):
                b = i - 2
                at_least(pool, s["ln2_stats"], b, 1, 1)
                at_least(pool, s["xn2_done"], b - 1, 1, 1)
                at_least(pool, s["xn2T_filled"], b - 1, 1, 1)
                at_least(pool, s["xn2_stored"], b - 1, 16, 16)
                normalise(x2, mv2, norm2, xn2, "xn2_done")
            if active(i - 1):
                b = i - 1
                at_least(pool, s["x_again_in"], b, 16, 16)
                at_least(pool, s["x2_done"], b - 1, 1, 1)
                nc.gpsimd.tensor_tensor(x_res[:], x_again[:],
                                        bo_all[:].unsqueeze(1).to_broadcast([P, QT, D]),
                                        ALU.add).then_inc(s["x_res_done"], 1)
            if active(i + 2):
                first_norm(i + 2)

        first_norm(0)
        run(pool, iteration)


def routing_program(nc, io, keep, ctx):
    def sb(name, shape, dt=F32):
        return ctx.enter_context(nc.sbuf_tensor(name, shape, dt))

    def sem(name):
        return ctx.enter_context(nc.semaphore(name))

    E, TE = EXPERTS, NT * EXPERTS
    PAIRS = 2 * NT
    RING = 8
    later = sb("later", [P, P], BF16)
    later_f = sb("later_f", [P, P])
    ones = sb("ones_bf", [P, P], BF16)
    consts = sb("consts", [P, io["consts"].shape[1]])
    put = {name: consts[:, a:b] for name, (a, b) in CONST_COLS.items()}
    expl, score, masked, tmp = (sb(n, [P, NT, E]) for n in ("expl", "score", "masked", "tmp"))
    top1, top2, comb, rank = (sb(n, [P, NT, E]) for n in ("top1", "top2", "comb", "rank"))
    col = {n: sb("col_" + n, [P, NT]) for n in ("max", "sum", "inv", "v1", "v2", "f", "w1", "w2")}
    picks = sb("picks", [P, NT, E], BF16)
    picks_sum = sb("picks_sum", [P, E])
    picks_sum_bf = sb("picks_sum_bf", [P, E], BF16)
    count, tiles, before, until, base = (sb(n, [P, E]) for n in ("count", "tiles", "before", "until", "base"))
    passed = sb("passed", [P, E, NT])
    tri = sb("tri_tmp", [P, E, E])
    slot = sb("slot", [P, PAIRS])
    slot_i, tile_i, lane_i = (sb(n, [P, PAIRS], I32) for n in ("slot_i", "tile_i", "lane_i"))
    tile_f, lane_f = (sb(n, [P, PAIRS]) for n in ("tile_f", "lane_f"))
    lane_hot = sb("lane_hot", [P, RING, P], F32R)
    tile_hot = sb("tile_hot", [P, RING, SLOT_COLS], F32R)
    slot_token, is_pad = (sb(n, [P, SLOT_COLS]) for n in ("slot_token", "is_pad"))
    owner = sb("owner", [P, SLOT_COLS, E - 1])
    gather_idx, scatter_idx, tile_expert = keep["gather_idx"], keep["scatter_idx"], keep["tile_expert"]
    w1_hi, w1_lo, w1_raw = keep["w1_hi"], keep["w1_lo"], keep["w1_raw"]
    wo_raw, wo_hi, wo_lo = sb("wo2_raw", [P, HID // P, D]), keep["wo_hi"], keep["wo_lo"]
    rank_ps = ctx.enter_context(nc.psum_tensor("rank_ps", [P, 512], F32))
    count_ps = ctx.enter_context(nc.psum_tensor("count_ps", [P, 512], F32))
    slot_ps = ctx.enter_context(nc.psum_tensor("slot_ps", [P, 512], F32))
    s = {n: sem("r_" + n) for n in (
        "consts_in wo_in b1_in w1_hi_done w1_lo_done wo_hi_done wo_lo_done dve_step "
        "exp_done picks_ready ones_ready counted ranked hot_ready hot_used slots_found comb_ready "
        "comb_stored max_taken").split()}
    w1_in = [sem(f"r_w1_in{e}") for e in range(E)]
    logits = keep["logits"][:].rearrange("p (t e) -> p t e", e=E)
    block = ctx.enter_context(nc.Block())

    @block.sync
    def _(sp):
        sp.dma_start(consts[:], io["consts"]).then_inc(s["consts_in"], 16)
        sp.dma_start(later_f[:], io["later"]).then_inc(s["consts_in"], 16)
        for e in range(E):
            sp.dma_start(w1_raw[:, :, e, :], io["W1T"].rearrange("(c p) e h -> p c e h", p=P)[:, :, e, :]
                         ).then_inc(w1_in[e], 16)
        sp.dma_start(wo_raw[:], io["WoT"].rearrange("(c p) n -> p c n", p=P)).then_inc(s["wo_in"], 16)
        sp.dma_start(keep["b1"][:], io["b1"].rearrange("e h -> (e h)").partition_broadcast(P)).then_inc(s["b1_in"], 16)
        sp.dma_start(keep["bo2"][:], io["bo2"].partition_broadcast(P)).then_inc(s["b1_in"], 16)
        sp.wait_ge(s["comb_ready"], 1)
        sp.dma_start(io["rows"][:, D:ROW].rearrange("(t p) e -> p t e", p=P), comb[:]).then_inc(s["comb_stored"], 16)
        sp.wait_ge(s["comb_stored"], 16)
        sp.wait_ge(s["b1_in"], 32)

    @block.scalar
    def _(act):
        act.wait_ge(s["max_taken"], 1)
        nc.scalar.activation(expl[:], masked[:], ACT.Exp).then_inc(s["exp_done"], 1)
        for e in range(E):
            act.wait_ge(w1_in[e], 16)
            nc.scalar.activation(w1_hi[:, :, e, :], w1_raw[:, :, e, :], ACT.Copy).then_inc(s["w1_hi_done"], 1)
        act.wait_ge(s["wo_in"], 16)
        nc.scalar.activation(wo_hi[:], wo_raw[:], ACT.Copy).then_inc(s["wo_hi_done"], 1)

    @block.gpsimd
    def _(pool):
        for e in range(E):
            pool.wait_ge(s["w1_hi_done"], e + 1)
            nc.gpsimd.tensor_tensor(w1_lo[:, :, e, :], w1_raw[:, :, e, :], w1_hi[:, :, e, :].bitcast(F32),
                                    ALU.subtract).then_inc(s["w1_lo_done"], 1)
        pool.wait_ge(s["wo_hi_done"], 1)
        nc.gpsimd.tensor_tensor(wo_lo[:], wo_raw[:], wo_hi[:].bitcast(F32), ALU.subtract).then_inc(s["wo_lo_done"], 1)

    @block.tensor
    def _(pe):
        pe.wait_ge(s["ones_ready"], 1)
        pe.wait_ge(s["picks_ready"], 2)
        nc.tensor.matmul(count_ps[:, 0:E], ones[:], picks_sum_bf[:], start=True, stop=True).then_inc(s["counted"], 1)
        flat = picks[:].rearrange("p t e -> p (t e)")
        nc.tensor.matmul(rank_ps[:, 0:TE], later[:], flat, start=True, stop=False)
        for back in range(1, NT):
            last = nc.tensor.matmul(rank_ps[:, back * E:TE], ones[:], flat[:, 0:TE - back * E],
                                    start=False, stop=(back == NT - 1))
        last.then_inc(s["ranked"], 1)
        for c in range(PAIRS):
            pe.wait_ge(s["hot_ready"], c + 1)
            nc.tensor.matmul(slot_ps[:, 0:SLOT_COLS], lane_hot[:, c % RING, :], tile_hot[:, c % RING, :],
                             start=(c == 0), stop=(c == PAIRS - 1)).then_inc(s["hot_used"], 1)

    @block.vector
    def _(dve):
        steps = [0]

        def then(ins):
            steps[0] += 1
            ins.then_inc(s["dve_step"], 1)
            dve.wait_ge(s["dve_step"], steps[0])

        def by_token(column):
            return column.unsqueeze(2).to_broadcast([P, NT, E])

        tt, ts, red = nc.vector.tensor_tensor, nc.vector.tensor_scalar, nc.vector.tensor_reduce
        then(red(col["max"][:], logits, AX.X, ALU.max))
        tt(masked[:], logits, by_token(col["max"][:]), ALU.subtract).then_inc(s["max_taken"], 1)
        dve.wait_ge(s["consts_in"], 32)
        then(nc.vector.tensor_copy(later[:], later_f[:]))
        nc.vector.memset(ones[:], 1.0).then_inc(s["ones_ready"], 1)
        dve.wait_ge(s["exp_done"], 1)
        then(red(col["sum"][:], expl[:], AX.X, ALU.add))
        then(nc.vector.reciprocal(col["inv"][:], col["sum"][:]))
        then(tt(score[:], expl[:], by_token(col["inv"][:]), ALU.mult))

        def first_best(values, best, pick):
            then(red(best[:], values[:], AX.X, ALU.max))
            then(tt(tmp[:], values[:], by_token(best[:]), ALU.is_equal))
            then(tt(tmp[:], tmp[:], put["falling"].unsqueeze(1).to_broadcast([P, NT, E]), ALU.mult))
            then(red(col["f"][:], tmp[:], AX.X, ALU.max))
            then(tt(pick[:], tmp[:], by_token(col["f"][:]), ALU.is_equal))

        first_best(score, col["v1"], top1)
        then(nc.vector.scalar_tensor_tensor(out=masked[:], in0=top1[:], scalar=-2.0, in1=score[:],
                                            op0=ALU.mult, op1=ALU.add))
        first_best(masked, col["v2"], top2)
        then(tt(tmp[:], top1[:], top2[:], ALU.add))
        nc.vector.tensor_copy(picks[:], tmp[:]).then_inc(s["picks_ready"], 1)
        then(red(picks_sum[:], tmp[:].rearrange("p t e -> p e t"), AX.X, ALU.add))
        nc.vector.tensor_copy(picks_sum_bf[:], picks_sum[:]).then_inc(s["picks_ready"], 1)
        then(tt(col["sum"][:], col["v1"][:], col["v2"][:], ALU.add))
        then(ts(col["sum"][:], col["sum"][:], TOP_EPS, None, ALU.add))
        then(nc.vector.reciprocal(col["inv"][:], col["sum"][:]))
        then(tt(col["w1"][:], col["v1"][:], col["inv"][:], ALU.mult))
        then(tt(col["w2"][:], col["v2"][:], col["inv"][:], ALU.mult))
        then(tt(comb[:], top1[:], by_token(col["w1"][:]), ALU.mult))
        then(tt(masked[:], top2[:], by_token(col["w2"][:]), ALU.mult))
        tt(comb[:], comb[:], masked[:], ALU.add).then_inc(s["comb_ready"], 1)
        dve.wait_ge(s["counted"], 1)
        then(nc.vector.tensor_copy(count[:], count_ps[:, 0:E]))
        then(tt(passed[:], count[:].unsqueeze(2).to_broadcast([P, E, NT]),
                put["tile_starts"].unsqueeze(1).to_broadcast([P, E, NT]), ALU.is_gt))
        then(red(tiles[:], passed[:], AX.X, ALU.add))
        then(tt(tri[:], tiles[:].unsqueeze(1).to_broadcast([P, E, E]),
                put["below"].rearrange("p (a b) -> p a b", b=E), ALU.mult))
        then(red(before[:], tri[:], AX.X, ALU.add))
        then(tt(until[:], before[:], tiles[:], ALU.add))
        then(ts(base[:], before[:], float(P), None, ALU.mult))
        then(tt(owner[:], put["numbers"][:, 0:SLOT_COLS].unsqueeze(2).to_broadcast([P, SLOT_COLS, E - 1]),
                until[:, 0:E - 1].unsqueeze(1).to_broadcast([P, SLOT_COLS, E - 1]), ALU.is_ge))
        then(red(slot_token[:], owner[:], AX.X, ALU.add))
        then(nc.vector.tensor_copy(tile_expert[:], slot_token[:]))
        dve.wait_ge(s["ranked"], 1)
        then(tt(rank[:], rank_ps[:, 0:TE].rearrange("p (t e) -> p t e", e=E),
                base[:].unsqueeze(1).to_broadcast([P, NT, E]), ALU.add))
        for n, top in enumerate((top1, top2)):
            then(tt(tmp[:], top[:], rank[:], ALU.mult))
            then(red(slot[:, n * NT:(n + 1) * NT], tmp[:], AX.X, ALU.add))
        then(nc.vector.tensor_copy(slot_i[:], slot[:]))
        then(ts(tile_i[:], slot_i[:], 7, None, ALU.arith_shift_right))
        then(ts(lane_i[:], slot_i[:], P - 1, None, ALU.bitwise_and))
        then(nc.vector.tensor_copy(tile_f[:], tile_i[:]))
        then(nc.vector.tensor_copy(lane_f[:], lane_i[:]))
        for c in range(PAIRS):
            if c >= RING:
                dve.wait_ge(s["hot_used"], c - RING + 1)
            ts(lane_hot[:, c % RING, :], put["numbers"], lane_f[:, c:c + 1], None, ALU.is_equal)
            ts(tile_hot[:, c % RING, :], put["numbers"][:, 0:SLOT_COLS], tile_f[:, c:c + 1],
               put["token"][:, c % NT:c % NT + 1], ALU.is_equal, ALU.mult).then_inc(s["hot_ready"], 1)
        dve.wait_ge(s["hot_used"], PAIRS)
        then(nc.vector.tensor_copy(slot_token[:], slot_ps[:, 0:SLOT_COLS]))
        then(ts(is_pad[:], slot_token[:], 0.0, None, ALU.is_equal))
        then(ts(is_pad[:], is_pad[:], put["spare_row"], None, ALU.mult))
        then(ts(slot_token[:], slot_token[:], -1.0, None, ALU.add))
        then(tt(is_pad[:], is_pad[:], slot_token[:], ALU.add))
        then(nc.vector.tensor_copy(scatter_idx[:], is_pad[:]))
        then(ts(slot_token[:], slot_token[:], 0.0, None, ALU.max))
        then(nc.vector.tensor_copy(gather_idx[:], slot_token[:]))


SLOT_COLS = SLOT_TILES + SLOT_TILES % 2
CONST_COLS, _at = {}, 0
for _name, _n in (("falling", EXPERTS), ("below", EXPERTS * EXPERTS), ("tile_starts", NT),
                  ("numbers", P), ("token", NT), ("spare_row", 1)):
    CONST_COLS[_name] = (_at, _at + _n)
    _at += _n


def constants():
    one = np.ones((P, 1), np.float32)
    lane = np.arange(P, dtype=np.float32)[:, None]
    e = np.arange(EXPERTS)
    return np.concatenate([
        one * (EXPERTS - e),
        one * (e[None, :] < e[:, None]).reshape(1, -1),
        one * (P * np.arange(NT)),
        one * np.arange(P),
        lane + P * np.arange(NT) + 1,
        lane + TOKENS + 1,
    ], axis=1).astype(np.float32)


def expert_program(nc, io, keep, ctx):
    def sb(name, shape, dt=F32):
        return ctx.enter_context(nc.sbuf_tensor(name, shape, dt))

    def sem(name):
        return ctx.enter_context(nc.semaphore(name))

    HC = HID // P
    ident, w1_hi, w1_lo, wo_hi, wo_lo = (keep[n] for n in ("ident", "w1_hi", "w1_lo", "wo_hi", "wo_lo"))
    b1, bo2, tile_expert = keep["b1"], keep["bo2"], keep["tile_expert"]
    rows = [sb(f"rows{p}", [P, ROW]) for p in range(2)]
    from_rows = [sb(f"from_rows{p}", [P, 1], U32) for p in range(2)]
    to_rows = [sb(f"to_rows{p}", [P, 1], U32) for p in range(2)]
    weight = sb("weight", [P, SLOT_COLS])
    xT_hi = [sb(f"xT_hi{p}", [P, KC, P], F32R) for p in range(2)]
    xT_lo = [sb(f"xT_lo{p}", [P, KC, P], F32R) for p in range(2)]
    gate_in, sig, up = sb("gate_in", [P, HID]), sb("sig", [P, HID]), sb("up", [P, HID])
    g = sb("g", [P, HID])
    gT_hi, gT_lo = sb("gT_hi", [P, HC, P], F32R), sb("gT_lo", [P, HC, P], F32R)
    y_biased = sb("y_biased", [P, D])
    y = [sb(f"y{p}", [P, D]) for p in range(2)]
    hb_ps = ctx.enter_context(nc.psum_tensor("hb_ps", [P, 2, 512], F32))
    ha_ps = ctx.enter_context(nc.psum_tensor("ha_ps", [P, 2, 512], F32))
    y_ps = ctx.enter_context(nc.psum_tensor("y_ps", [P, 2, 512], F32))
    xT_ps = ctx.enter_context(nc.psum_tensor("xT_ps", [P, 512], F32))
    gT_ps = ctx.enter_context(nc.psum_tensor("gT_ps", [P, 512], F32))
    s = {n: sem("e_" + n) for n in (
        "xT_filled xT_hi_done xT_lo_done weight_saved hb_filled ha_filled gate_in_done "
        "sig_done up_done g_done gT_filled gT_hi_done gT_lo_done y_filled y_biased_done y_done "
        "gathers_begun scatters_begun from_rows_set to_rows_set scattered").split()}

    def active(t, lag):
        return not isinstance(t, int) or 0 <= t + lag < SLOT_TILES

    def past(eng, sem_, t):
        at_least(eng, sem_, t, 1, 1)

    def run(eng, iteration):
        for t in range(-1, 4):
            iteration(t, t % 2)
        with eng.Fori(2, (SLOT_TILES - 3) // 2) as pair:
            iteration(pair * 2, 0)
            iteration(pair * 2 + 1, 1)
        for t in range((SLOT_TILES - 3) // 2 * 2, SLOT_TILES + 2):
            iteration(t, t % 2)

    gathered = [sem(f"e_gathered{p}") for p in range(2)]

    def rows_there(eng, t, par):
        at_least(eng, gathered[par], t - par, 8, 16)

    def expert_of(eng, t):
        return eng.value_load(tile_expert[0:1, bass.ds(t, 1)], min_val=0, max_val=EXPERTS - 1)

    block = ctx.enter_context(nc.Block())

    @block.gpsimd
    def _(pool):
        def gather(t, par):
            past(pool, s["xT_filled"], t - 2)
            past(pool, s["weight_saved"], t - 2)
            rows_there(pool, t - 2, par)
            nc.gpsimd.tensor_copy(from_rows[par][:], keep["gather_idx"][:, bass.ds(t, 1)]
                                  ).then_inc(s["from_rows_set"], 1)
            past(pool, s["from_rows_set"], t)
            pool.sem_inc(s["gathers_begun"], 1)
            nc.gpsimd.indirect_dma_start(
                out=rows[par][:], out_offset=None, in_=io["rows"],
                in_offset=bass.IndirectOffsetOnAxis(ap=from_rows[par][:], axis=0)
            ).then_inc(gathered[par], 16)

        def iteration(t, par):
            if active(t, 2):
                gather(t + 2, par)
            if active(t, -2):
                at_least(pool, s["scattered"], t - 4, 16, 16)
                nc.gpsimd.tensor_copy(to_rows[par][:], keep["scatter_idx"][:, bass.ds(t - 2, 1)]
                                      ).then_inc(s["to_rows_set"], 1)
                past(pool, s["to_rows_set"], t - 2)
                past(pool, s["y_done"], t - 2)
                at_least(pool, s["scattered"], t - 3, 16, 16)
                pool.sem_inc(s["scatters_begun"], 1)
                nc.gpsimd.indirect_dma_start(
                    out=io["out"], in_=y[par][:], in_offset=None, compute_op=ALU.add,
                    out_offset=bass.IndirectOffsetOnAxis(ap=to_rows[par][:], axis=0)
                ).then_inc(s["scattered"], 16)

        gather(0, 0)
        run(pool, iteration)
        pool.wait_ge(s["scattered"], 16 * SLOT_TILES)

    @block.tensor
    def _(pe):
        def first_product(t, par, e, half, out, filled):
            first = True
            for c in range(KC):
                cols = bass.ds(e * (2 * HID) + half * HID, HID)
                w_hi, w_lo = (w[:, c].rearrange("p e h -> p (e h)")[:, cols] for w in (w1_hi, w1_lo))
                nc.tensor.matmul(out, xT_hi[par][:, c, :], w_hi, start=first, stop=False)
                nc.tensor.matmul(out, xT_hi[par][:, c, :], w_lo, start=False, stop=False)
                last = nc.tensor.matmul(out, xT_lo[par][:, c, :], w_hi, start=False, stop=(c == KC - 1))
                first = False
            last.then_inc(s[filled], 1)

        def iteration(t, par):
            other = (par + 1) % 2
            if active(t, 0):
                e = expert_of(pe, t)
                past(pe, s["xT_lo_done"], t)
                past(pe, s["gate_in_done"], t - 2)
                first_product(t, par, e, 1, hb_ps[:, par, :], "hb_filled")
            if active(t, -1):
                past(pe, s["g_done"], t - 1)
                past(pe, s["gT_lo_done"], t - 2)
                for c in range(HC):
                    last = nc.tensor.transpose(gT_ps[:, c * P:(c + 1) * P], g[:, c * P:(c + 1) * P], ident[:])
                last.then_inc(s["gT_filled"], 1)
            if active(t, 0):
                past(pe, s["up_done"], t - 2)
                first_product(t, par, e, 0, ha_ps[:, par, :], "ha_filled")
            if active(t, 1):
                rows_there(pe, t + 1, other)
                past(pe, s["xT_lo_done"], t)
                for c in range(KC):
                    last = nc.tensor.transpose(xT_ps[:, c * P:(c + 1) * P],
                                               rows[other][:, c * P:(c + 1) * P], ident[:])
                last.then_inc(s["xT_filled"], 1)
            if active(t, -1):
                past(pe, s["gT_lo_done"], t - 1)
                past(pe, s["y_biased_done"], t - 3)
                out = y_ps[:, other, 0:D]
                for c in range(HC):
                    nc.tensor.matmul(out, gT_hi[:, c, :], wo_hi[:, c, :], start=(c == 0), stop=False)
                    nc.tensor.matmul(out, gT_hi[:, c, :], wo_lo[:, c, :], start=False, stop=False)
                    last = nc.tensor.matmul(out, gT_lo[:, c, :], wo_hi[:, c, :], start=False, stop=(c == HC - 1))
                last.then_inc(s["y_filled"], 1)

        run(pe, iteration)

    @block.scalar
    def _(act):
        def iteration(t, par):
            other = (par + 1) % 2
            if active(t, -2):
                past(act, s["y_biased_done"], t - 2)
                at_least(act, s["scattered"], t - 4, 16, 16)
                nc.scalar.activation(y[par][:], y_biased[:], ACT.Copy,
                                     scale=weight[:, bass.ds(t - 2, 1)]).then_inc(s["y_done"], 1)
            if active(t, -1):
                past(act, s["gT_filled"], t - 1)
                past(act, s["y_filled"], t - 2)
                nc.scalar.activation(gT_hi[:].rearrange("p c t -> p (c t)"), gT_ps[:], ACT.Copy
                                     ).then_inc(s["gT_hi_done"], 1)
            if active(t, 0):
                past(act, s["gate_in_done"], t)
                past(act, s["g_done"], t - 1)
                nc.scalar.activation(sig[:], gate_in[:], ACT.Sigmoid).then_inc(s["sig_done"], 1)
            if active(t, 1):
                past(act, s["xT_filled"], t + 1)
                past(act, s["ha_filled"], t - 1)
                nc.scalar.activation(xT_hi[other][:].rearrange("p c t -> p (c t)"), xT_ps[:, 0:KC * P],
                                     ACT.Copy).then_inc(s["xT_hi_done"], 1)

        run(act, iteration)

    @block.vector
    def _(dve):
        def iteration(t, par):
            other = (par + 1) % 2
            if active(t, -2):
                past(dve, s["y_filled"], t - 2)
                past(dve, s["y_done"], t - 3)
                nc.vector.tensor_tensor(y_biased[:], y_ps[:, par, 0:D], bo2[:], ALU.add
                                        ).then_inc(s["y_biased_done"], 1)
            if active(t, 0):
                e = expert_of(dve, t)
                past(dve, s["hb_filled"], t)
                past(dve, s["sig_done"], t - 1)
                nc.vector.tensor_tensor(gate_in[:], hb_ps[:, par, :], b1[:, bass.ds(e * (2 * HID) + HID, HID)],
                                        ALU.add).then_inc(s["gate_in_done"], 1)
            if active(t, -1):
                past(dve, s["gT_hi_done"], t - 1)
                past(dve, s["y_filled"], t - 2)
                nc.vector.tensor_tensor(gT_lo[:].rearrange("p c t -> p (c t)"), gT_ps[:],
                                        gT_hi[:].rearrange("p c t -> p (c t)").bitcast(F32),
                                        ALU.subtract).then_inc(s["gT_lo_done"], 1)
            if active(t, 0):
                past(dve, s["ha_filled"], t)
                past(dve, s["g_done"], t - 1)
                nc.vector.tensor_tensor(up[:], ha_ps[:, par, :], b1[:, bass.ds(e * (2 * HID), HID)],
                                        ALU.add).then_inc(s["up_done"], 1)
                past(dve, s["up_done"], t)
                past(dve, s["sig_done"], t)
                past(dve, s["gT_filled"], t - 1)
                nc.vector.tensor_tensor(g[:], up[:], sig[:], ALU.mult).then_inc(s["g_done"], 1)
            if active(t, 1):
                e_next = expert_of(dve, t + 1)
                rows_there(dve, t + 1, other)
                nc.vector.tensor_copy(weight[:, bass.ds(t + 1, 1)], rows[other][:, bass.ds(e_next + D, 1)]
                                      ).then_inc(s["weight_saved"], 1)
                past(dve, s["xT_hi_done"], t + 1)
                past(dve, s["ha_filled"], t - 1)
                nc.vector.tensor_tensor(xT_lo[other][:].rearrange("p c t -> p (c t)"), xT_ps[:, 0:KC * P],
                                        xT_hi[other][:].rearrange("p c t -> p (c t)").bitcast(F32),
                                        ALU.subtract).then_inc(s["xT_lo_done"], 1)

        run(dve, iteration)


def build(nc, io, phases=3):
    with ExitStack() as ctx:
        keep = {"ident": ctx.enter_context(nc.sbuf_tensor("ident", [P, P], F32)),
                "logits": ctx.enter_context(nc.sbuf_tensor("logits", [P, NT * EXPERTS], F32))}
        with ExitStack() as stage:
            attention_program(nc, io, keep, stage)
        if phases >= 2:
            hold = lambda name, shape, dt=F32: ctx.enter_context(nc.sbuf_tensor(name, shape, dt))
            with nc.sbuf_tensor("w1_raw", [P, KC, EXPERTS, 2 * HID], F32) as w1_raw:
                keep["w1_raw"] = w1_raw
            keep["w1_lo"] = hold("w1_lo", [P, KC, EXPERTS, 2 * HID], F32R)
            keep["w1_hi"] = hold("w1_hi", [P, KC, EXPERTS, 2 * HID], F32R)
            keep["wo_hi"] = hold("wo2_hi", [P, HID // P, D], F32R)
            keep["wo_lo"] = hold("wo2_lo", [P, HID // P, D], F32R)
            keep["b1"] = hold("b1_all", [P, EXPERTS * 2 * HID])
            keep["bo2"] = hold("bo2_all", [P, D])
            keep["gather_idx"] = hold("gather_idx", [P, SLOT_COLS], U32)
            keep["scatter_idx"] = hold("scatter_idx", [P, SLOT_COLS], U32)
            keep["tile_expert"] = hold("tile_expert", [P, SLOT_COLS], I32)
            with ExitStack() as stage:
                routing_program(nc, io, keep, stage)
            if phases == 3:
                with ExitStack() as stage:
                    expert_program(nc, io, keep, stage)
        if phases == 1:
            dsem = ctx.enter_context(nc.semaphore("dbg"))
            with nc.Block() as block:
                @block.sync
                def _(sp):
                    sp.dma_start(io["dbg"], keep["logits"][:]).then_inc(dsem, 16)
                    sp.wait_ge(dsem, 16)


def layouts(inputs):
    g = {k: np.asarray(v) for k, v in inputs.items()}
    heads_last = np.arange(D).reshape(KC, D // KC // HD, HD).transpose(0, 2, 1).reshape(-1)
    for n in ("Wq", "Wk", "bq", "bk"):
        g["L0_xattn_" + n] = np.ascontiguousarray(g["L0_xattn_" + n][..., heads_last])
    return {
        "x": g["x"], "ctx": g["ctx_1024"],
        "Wq": g["L0_xattn_Wq"], "Wk": g["L0_xattn_Wk"], "Wv": g["L0_xattn_Wv"], "Wo": g["L0_xattn_Wo"],
        "bq": g["L0_xattn_bq"], "bk": g["L0_xattn_bk"], "bv": g["L0_xattn_bv"], "bo": g["L0_xattn_bo"],
        "WgT": np.ascontiguousarray(g["L0_ffn_Wg"].T),
        "W1T": np.ascontiguousarray(g["L0_ffn_W1"].transpose(2, 0, 1)),
        "b1": g["L0_ffn_b1"], "WoT": np.ascontiguousarray(g["L0_ffn_Wo"].T), "bo2": g["L0_ffn_bo"],
        "ident": np.eye(P, dtype=np.float32),
        "later": np.triu(np.ones((P, P), np.float32), 1),
        "consts": constants(),
    }


def kernel(**inputs):
    import concourse.bacc as bacc
    from concourse.bass_utils import run_bass_kernel_spmd

    arrays = {f"in_{name}": a for name, a in layouts(inputs).items()}
    nc = bacc.Bacc("TRN2", target_bir_lowering=False, num_devices=1)
    io = {name[3:]: nc.dram_tensor(name, a.shape, mybir.dt.from_np(a.dtype), kind="ExternalInput").ap()
          for name, a in arrays.items()}
    io["out"] = nc.dram_tensor("out_rows", (TOKENS + P, D), F32, kind="ExternalOutput").ap()
    io["rows"] = nc.dram_tensor("token_rows", (TOKENS, ROW), F32, kind="Internal").ap()
    build(nc, io)
    r = run_bass_kernel_spmd(nc, [arrays], core_ids=[0])
    return r.results[0]["out_rows"][0:TOKENS].reshape(BATCH, TOK, D)
```

```python
from contextlib import ExitStack

import concourse.bass as bass
import numpy as np
from concourse import mybir

F32 = mybir.dt.float32
F32R = mybir.dt.float32r
BF16 = mybir.dt.bfloat16
I32 = mybir.dt.int32
U32 = mybir.dt.uint32
ALU = mybir.AluOpType
ACT = mybir.ActivationFunctionType
AX = mybir.AxisListType

P = 128
BATCH = 16
TOK = 256
D = 256
HEADS = 16
HD = D // HEADS
KC = D // P
QT = TOK // P
QUAD = 4
NQ = HEADS // QUAD
NT = BATCH * QT
TOKENS = BATCH * TOK
EXPERTS = 8
HID = 512
ROW = D + EXPERTS
SLOT_TILES = (2 * TOKENS + EXPERTS * (P - 1)) // P
EPS = 1e-5
TOP_EPS = 1e-9
MAGIC = 1597463007.0
NEWTON_STEPS = 3
M_ROW = 3 * HD


def at_least(eng, sem, tile, per_tile, nth):
    if isinstance(tile, int) and tile < 0:
        return
    eng.wait_ge(sem, tile * per_tile + nth)


def expert_w1(io, e):
    return io["W1T"].rearrange("(c p) e h -> p c e h", p=P)[:, :, e, :]


def attention_program(nc, io, keep, ctx):
    def sb(name, shape, dt=F32):
        return ctx.enter_context(nc.sbuf_tensor(name, shape, dt))

    def sem(name):
        return ctx.enter_context(nc.semaphore(name))

    qs = [sb(f"q_stack{p}", [P, HEADS, TOK], F32R) for p in range(2)]
    ks = [sb(f"k_stack{p}", [P, HEADS, TOK], F32R) for p in range(2)]
    ident = keep["ident"]
    w_raw = sb("w_raw", [P, 4, KC, D])
    w_hi = sb("w_hi", [P, 4, KC, D], F32R)
    w_lo = sb("w_lo", [P, 4, KC, D], F32R)
    WQ, WK, WV, WO = range(4)
    wg = sb("wg", [P, KC, EXPERTS])
    bqk = sb("bqk", [P, 2, KC])
    bv_all = sb("bv_all", [P, D])
    bo_all = sb("bo_all", [P, D])
    zeros = sb("zeros", [HEADS, TOK])
    ones = sb("ones", [HEADS, TOK])
    x_rows = sb("x_rows", [P, QT, D])
    ctxT = sb("ctxT", [P, KC, TOK])
    xn = sb("xn", [P, QT, D])
    ctxT_hi = sb("ctxT_hi", [P, KC, TOK], F32R)
    ctxT_lo = sb("ctxT_lo", [P, KC, TOK], F32R)
    xT_hi = sb("xT_hi", [P, KC, TOK], F32R)
    xT_lo = sb("xT_lo", [P, KC, TOK], F32R)
    q_hi = sb("q_hi", [P, KC, TOK], F32R)
    q_lo = sb("q_lo", [P, KC, TOK], F32R)
    k_hi = sb("k_hi", [P, KC, TOK], F32R)
    k_lo = sb("k_lo", [P, KC, TOK], F32R)
    vals = [sb(f"values{p}", [P, QT, HEADS, 2 * HD]) for p in range(2)]
    neg_max = sb("neg_max", [P, QT, HEADS])
    m_row = sb("m_row", [QUAD, NQ, TOK], F32R)
    probs = sb("probs", [P, 8, QT * TOK])
    quad_sb = sb("quad_sb", [P, NQ, TOK])
    recip = sb("recip", [P, QT, HEADS])
    attn = sb("attn", [P, QT, D])
    attnT_hi = sb("attnT_hi", [P, KC, TOK], F32R)
    attnT_lo = sb("attnT_lo", [P, KC, TOK], F32R)
    x_again = sb("x_again", [P, QT, D])
    x_res = sb("x_res", [P, QT, D])
    x2 = sb("x2", [P, QT, D])
    xn2 = sb("xn2", [P, QT, D])
    xn2T = sb("xn2T", [P, KC, TOK])
    eps = sb("eps", [P, QT])
    stats1 = sb("stats1", [P, QT, 6])
    stats2 = sb("stats2", [P, QT, 6])
    mv1 = sb("mv1", [P, QT, 2])
    mv2 = sb("mv2", [P, QT, 2])
    norm1 = sb("norm1", [P, 4, QT])
    norm2 = sb("norm2", [P, 4, QT])
    logits = keep["logits"]

    st = ctx.enter_context(nc.psum_tensor("scoresT", [P, 2, QT * TOK], F32))
    mx = ctx.enter_context(nc.psum_tensor("scores", [P, 2, QT * TOK], F32))
    ov = ctx.enter_context(nc.psum_tensor("quads_out", [P, 2, TOK], F32))
    misc = ctx.enter_context(nc.psum_tensor("misc", [P, 3, 512], F32))

    s = {n: sem("a_" + n) for n in (
        "ident_in weights_in w_hi_done w_lo_done bias_done first_k_cleared cleared values_cleared ones_set "
        "x_in ctx_in x_again_in k_stacked q_stacked x2_stored xn2_stored "
        "xT_filled k_filled q_filled v_filled mT_filled scores_filled scoresT_filled "
        "pv_filled oT_filled attnT_filled proj_filled xn2T_filled gate_filled "
        "ctxT_hi_done xT_hi_done k_hi_done q_hi_done exp_done quad_saved attnT_hi_done xn2T_saved "
        "ctxT_lo_done xT_lo_done k_lo_done q_lo_done v_saved m_row_done max_done recip_done "
        "attn_done attnT_lo_done x2_done ln1_stats ln2_stats gate_saved "
        "xn_done x_res_done xn2_done").split()}
    m_placed = [sem(f"a_m_placed{p}") for p in range(2)]
    ones_placed = [sem(f"a_ones_placed{p}") for p in range(2)]
    WEIGHT_DMAS = 9 * 16
    K_DMAS, Q_DMAS = 3 * 16, 4 * 16

    x_dram = io["x"].rearrange("b (t p) d -> b p t d", p=P)
    ctx_dram = io["ctxT"].rearrange("b (c p) t -> b p c t", p=P)
    out_dram = io["out"][0:TOKENS, :].rearrange("(b t p) d -> b p t d", p=P, t=QT)
    xn2_dram = io["rows"][:, 0:D].rearrange("(b t p) d -> b p t d", p=P, t=QT)

    def active(b):
        return not isinstance(b, int) or 0 <= b < BATCH

    def at(i, n):
        return isinstance(i, int) and i == n

    def at_least(eng, sem, b, per_row, nth):
        if active(b):
            eng.wait_ge(sem, b * per_row + nth)

    EXP_LAG = 10
    PV_FIRST = EXP_LAG + QUAD + 1
    PV_STEPS = {PV_FIRST + QUAD * g - HEADS: g for g in range(1, NQ)}

    BANKS = ({"attnT": -2, "k": 1, "v": 1, "oT1": -1},
             {"proj": -2, "xT": 1, "q": 1, "oT0": -1},
             {"m3": -1, "m0": 0, "m1": 0, "xn2T": -2, "m2": 0, "gate": -2})
    ROW_OF = {name: lag for fills in BANKS for name, lag in fills.items()}
    BANK = {name: n for n, fills in enumerate(BANKS) for name in fills}

    def bank(name):
        return misc[:, BANK[name], :]

    def run(eng, iteration):
        for i in range(-1, 4):
            iteration(i, i % 2)
        with eng.Fori(2, 7) as pair:
            iteration(pair * 2, 0)
            iteration(pair * 2 + 1, 1)
        for i in (14, 15, 16, 17, 18):
            iteration(i, i % 2)

    block = ctx.enter_context(nc.Block())

    @block.sync
    def _(sp):
        sp.dma_start(x_rows[:], x_dram[0]).then_inc(s["x_in"], 16)
        sp.dma_start(ident[:], io["ident"]).then_inc(s["ident_in"], 16)
        sp.dma_start(ctxT[:], ctx_dram[0]).then_inc(s["ctx_in"], 16)
        for n, b in enumerate(("bq", "bk")):
            sp.dma_start(bqk[:, n], io[b].rearrange("(c p) -> p c", p=P),
                         allow_slow_non_contiguous=True).then_inc(s["weights_in"], 16)
        for n, w in enumerate(("Wq", "Wk", "Wv", "Wo")):
            sp.dma_start(w_raw[:, n], io[w].rearrange("(c p) n -> p c n", p=P)).then_inc(s["weights_in"], 16)
        sp.dma_start(wg[:], io["WgT"].rearrange("(c p) n -> p c n", p=P)).then_inc(s["weights_in"], 16)
        sp.dma_start(bv_all[:], io["bv"].partition_broadcast(P)).then_inc(s["weights_in"], 16)
        sp.dma_start(bo_all[:], io["bo"].partition_broadcast(P)).then_inc(s["weights_in"], 16)

        def stack(par, name, natural, dst, part):
            to = dst[par][part * HD:(part + 1) * HD]
            sp.dma_start(to.bitcast(F32), natural[:].bitcast(F32)).then_inc(s[name], 16)

        def place_m(i, par, lag, g):
            b = i + lag
            at_least(sp, s["m_row_done"], b, NQ, g + 1)
            sp.dma_start(qs[(par + lag) % 2][M_ROW:M_ROW + 1, QUAD * g:QUAD * (g + 1), :].bitcast(F32),
                         m_row[:, g, :].bitcast(F32)).then_inc(m_placed[g % 2], 16)

        def iteration(i, par):
            nxt = (par + 1) % 2
            if active(i + 2):
                at_least(sp, s["xn_done"], i + 1, 1, 1)
                sp.dma_start(x_rows[:], x_dram[i + 2]).then_inc(s["x_in"], 16)
            if active(i - 1):
                place_m(i, par, -1, 3)
            if active(i + 2):
                at_least(sp, s["ctxT_lo_done"], i + 1, 1, 1)
                sp.dma_start(ctxT[:], ctx_dram[i + 2]).then_inc(s["ctx_in"], 16)
            if active(i - 1):
                at_least(sp, s["x_res_done"], i - 2, 1, 1)
                sp.dma_start(x_again[:], x_dram[i - 1]).then_inc(s["x_again_in"], 16)
            if active(i - 2):
                at_least(sp, s["x2_done"], i - 2, 1, 1)
                sp.dma_start(out_dram[i - 2], x2[:]).then_inc(s["x2_stored"], 16)
            if active(i):
                place_m(i, par, 0, 0)
                place_m(i, par, 0, 1)
            if at(i, -1):
                sp.wait_ge(s["ones_set"], 1)
                sp.wait_ge(s["first_k_cleared"], 1)
                sp.wait_ge(s["cleared"], 1)
                sp.dma_start(ks[0][M_ROW:M_ROW + 1].bitcast(F32), ones[:]).then_inc(ones_placed[0], 16)
            if at(i, 0):
                sp.wait_ge(s["cleared"], 3)
                sp.dma_start(ks[1][M_ROW:M_ROW + 1].bitcast(F32), ones[:]).then_inc(ones_placed[1], 16)
            if active(i + 1):
                at_least(sp, s["scoresT_filled"], i - 1, HEADS, HEADS)
                at_least(sp, s["k_lo_done"], i + 1, 1, 1)
                stack(nxt, "k_stacked", k_hi, ks, 0)
                stack(nxt, "k_stacked", k_lo, ks, 1)
                stack(nxt, "k_stacked", k_hi, ks, 2)
            if active(i + 1):
                at_least(sp, s["q_lo_done"], i + 1, 1, 1)
                stack(nxt, "q_stacked", q_hi, qs, 0)
                stack(nxt, "q_stacked", q_hi, qs, 1)
                stack(nxt, "q_stacked", q_lo, qs, 2)
                sp.dma_start(qs[nxt][M_ROW:M_ROW + 1].bitcast(F32), zeros[:]).then_inc(s["q_stacked"], 16)
            if active(i - 2):
                at_least(sp, s["xn2_done"], i - 2, 1, 1)
                sp.dma_start(xn2_dram[i - 2], xn2[:]).then_inc(s["xn2_stored"], 16)
            if at(i, BATCH):
                sp.wait_ge(s["scoresT_filled"], BATCH * HEADS)
                for e in range(EXPERTS // 2):
                    sp.dma_start(keep["w1_raw"][:, :, e, :], expert_w1(io, e)).then_inc(keep["w1_in"][e], 16)
            if active(i):
                place_m(i, par, 0, 2)

        run(sp, iteration)
        sp.wait_ge(s["x2_stored"], 16 * BATCH)
        sp.wait_ge(s["xn2_stored"], 16 * BATCH)

    @block.tensor
    def _(pe):
        def three(out, lhs_hi, lhs_lo, rhs_hi, rhs_lo, first, last):
            nc.tensor.matmul(out, lhs_hi, rhs_hi, start=first, stop=False)
            nc.tensor.matmul(out, lhs_hi, rhs_lo, start=False, stop=False)
            return nc.tensor.matmul(out, lhs_lo, rhs_hi, start=False, stop=last)

        def transpose_rows(rows, out):
            for c in range(KC):
                for t in range(QT):
                    last = nc.tensor.transpose(out[:, c * TOK + t * P:c * TOK + (t + 1) * P],
                                               rows[:, t, c * P:(c + 1) * P], ident[:])
            return last

        def project_T(w, src_hi, src_lo, out):
            for m in range(KC):
                for c in range(KC):
                    cols = slice(m * P, (m + 1) * P)
                    last = three(out[:, m * TOK:(m + 1) * TOK], w_hi[:, w, c, cols], w_lo[:, w, c, cols],
                                 src_hi[:, c, :], src_lo[:, c, :], c == 0, c == KC - 1)
            return last

        def project(w, src_hi, src_lo, out):
            for t in range(QT):
                for c in range(KC):
                    cols = slice(t * P, (t + 1) * P)
                    last = three(out[:, t * D:(t + 1) * D], src_hi[:, c, cols], src_lo[:, c, cols],
                                 w_hi[:, w, c, :], w_lo[:, w, c, :], c == 0, c == KC - 1)
            return last

        def fill(i, name):
            b = i + ROW_OF[name]
            if not active(b):
                return
            out = bank(name)
            if name == "attnT":
                at_least(pe, s["attn_done"], b, 2, 2)
                transpose_rows(attn, out).then_inc(s["attnT_filled"], 1)
            elif name == "k":
                at_least(pe, s["v_saved"], i, 1, 1)
                at_least(pe, s["attnT_lo_done"], i - 2, 1, 1)
                at_least(pe, s["ctxT_lo_done"], b, 1, 1)
                project_T(WK, ctxT_hi, ctxT_lo, out).then_inc(s["k_filled"], 1)
            elif name == "v":
                at_least(pe, s["k_lo_done"], b, 1, 1)
                project(WV, ctxT_hi, ctxT_lo, out).then_inc(s["v_filled"], 1)
            elif name == "proj":
                at_least(pe, s["attnT_lo_done"], b, 1, 1)
                project(WO, attnT_hi, attnT_lo, out).then_inc(s["proj_filled"], 1)
            elif name == "xT":
                at_least(pe, s["x2_done"], i - 2, 1, 1)
                at_least(pe, s["xn_done"], b, 1, 1)
                transpose_rows(xn, out).then_inc(s["xT_filled"], 1)
            elif name == "q":
                at_least(pe, s["xT_lo_done"], b, 1, 1)
                project_T(WQ, xT_hi, xT_lo, out).then_inc(s["q_filled"], 1)
            elif name in ("oT0", "oT1"):
                t = int(name[2])
                if name == "oT0":
                    at_least(pe, s["x2_done"], i - 2, 1, 1)
                    at_least(pe, s["q_lo_done"], i + 1, 1, 1)
                    at_least(pe, s["quad_saved"], b, NQ // 2, NQ // 2)
                else:
                    at_least(pe, s["attnT_lo_done"], i - 2, 1, 1)
                    at_least(pe, s["v_saved"], i + 1, 1, 1)
                for g in range(NQ):
                    last = nc.tensor.transpose(out[:, g * P:(g + 1) * P],
                                               quad_sb[:, g, t * P:(t + 1) * P], ident[:])
                last.then_inc(s["oT_filled"], 1)
            elif name in ("m0", "m1", "m2", "m3"):
                g = int(name[1])
                if name == "m0":
                    at_least(pe, s["m_row_done"], i - 1, NQ, 4)
                elif name == "m1":
                    at_least(pe, s["m_row_done"], i, NQ, 1)
                elif name == "m2":
                    at_least(pe, s["m_row_done"], i, NQ, 2)
                    at_least(pe, s["xn2T_saved"], i - 2, 1, 1)
                else:
                    at_least(pe, s["m_row_done"], i - 1, NQ, 3)
                    at_least(pe, s["gate_saved"], i - 3, 1, 1)
                at_least(pe, s["max_done"], b, HEADS, QUAD * (g + 1))
                for t in range(QT):
                    last = nc.tensor.transpose(out[0:QUAD, t * P:(t + 1) * P],
                                               neg_max[:, t, QUAD * g:QUAD * (g + 1)], ident[:])
                last.then_inc(s["mT_filled"], 1)
            elif name == "xn2T":
                at_least(pe, s["m_row_done"], i, NQ, 2)
                at_least(pe, s["m_row_done"], i - 1, NQ, 4)
                at_least(pe, s["gate_saved"], i - 3, 1, 1)
                at_least(pe, s["xn2_done"], b, 1, 1)
                transpose_rows(xn2, out).then_inc(s["xn2T_filled"], 1)
            elif name == "gate":
                at_least(pe, s["m_row_done"], i, NQ, 3)
                at_least(pe, s["xn2T_saved"], b, 1, 1)
                for t in range(QT):
                    for c in range(KC):
                        last = nc.tensor.matmul(out[:, t * EXPERTS:(t + 1) * EXPERTS],
                                                xn2T[:, c, t * P:(t + 1) * P], wg[:, c, :],
                                                start=(c == 0), stop=(c == KC - 1))
                last.then_inc(s["gate_filled"], 1)

        def scores_for_max(i, par, h):
            if h == 0:
                if at(i, 0):
                    pe.wait_ge(s["values_cleared"], 4)
                    pe.wait_ge(ones_placed[0], 16)
                if at(i, 1):
                    pe.wait_ge(ones_placed[1], 16)
                at_least(pe, s["k_stacked"], i, K_DMAS, K_DMAS)
                at_least(pe, s["q_stacked"], i, Q_DMAS, Q_DMAS)
            at_least(pe, s["max_done"], i if h >= 2 else i - 1, HEADS, (h - 2) % HEADS + 1)
            for t in range(QT):
                last = nc.tensor.matmul(mx[:, h % 2, t * TOK:(t + 1) * TOK], qs[par][:, h, t * P:(t + 1) * P],
                                        ks[par][:, h, :], start=True, stop=True)
            last.then_inc(s["scores_filled"], 1)

        def scores_for_exp(b, par, h):
            if h % QUAD == 0:
                at_least(pe, m_placed[h // QUAD % 2], b, 16 * NQ // 2, 16 * (h // QUAD // 2 + 1))
            at_least(pe, s["exp_done"], b if h >= 2 else b - 1, HEADS, (h - 2) % HEADS + 1)
            for t in range(QT):
                last = nc.tensor.matmul(st[:, h % 2, t * TOK:(t + 1) * TOK], ks[par][:, h, t * P:(t + 1) * P],
                                        qs[par][:, h, :], start=True, stop=True)
            last.then_inc(s["scoresT_filled"], 1)

        def probs_times_values(b, par, g):
            at_least(pe, s["exp_done"], b, HEADS, QUAD * (g + 1))
            at_least(pe, s["v_saved"], b, 1, 1)
            if g % 2 == 0:
                at_least(pe, s["quad_saved"], b if g >= 2 else b - 1, NQ // 2, (g // 2 - 1) % (NQ // 2) + 1)
            for t in range(QT):
                for j in range(QUAD):
                    h = QUAD * g + j
                    last = nc.tensor.matmul(ov[32 * j:32 * (j + 1), g % 2, 0:TOK], vals[par][:, t, h, :],
                                            probs[:, h % 8, t * TOK:(t + 1) * TOK],
                                            start=(t == 0), stop=(t == QT - 1),
                                            tile_position=(0, 32 * j))
            last.then_inc(s["pv_filled"], 1)

        AT_STEP = {1: ["attnT"], 2: ["m3"], 3: ["proj"], 5: ["m0"], 6: ["xT"], 7: ["k"], 8: ["q"], 9: ["m1"],
                   10: ["v"], 12: ["oT0", "xn2T"], 14: ["m2", "oT1"], 15: ["gate"]}

        def iteration(i, par):
            for step in range(HEADS):
                if step < EXP_LAG and active(i - 1):
                    scores_for_exp(i - 1, (par + 1) % 2, step + HEADS - EXP_LAG)
                if step >= EXP_LAG and active(i):
                    scores_for_exp(i, par, step - EXP_LAG)
                if step in PV_STEPS and active(i - 1):
                    probs_times_values(i - 1, (par + 1) % 2, PV_STEPS[step])
                if step == PV_FIRST and active(i):
                    probs_times_values(i, par, 0)
                if active(i):
                    scores_for_max(i, par, step)
                if at(i, -1) and step == 7:
                    pe.wait_ge(s["w_lo_done"], 4)
                for name in AT_STEP.get(step, []):
                    fill(i, name)

        pe.wait_ge(s["ident_in"], 16)
        run(pe, iteration)

    @block.scalar
    def _(act):
        act.wait_ge(s["weights_in"], WEIGHT_DMAS)
        for n in range(4):
            nc.scalar.activation(w_hi[:, n], w_raw[:, n], ACT.Copy,
                                 scale=0.25 if n == WQ else 1.0).then_inc(s["w_hi_done"], 1)

        def hi(name, dst, done):
            nc.scalar.activation(dst[:].rearrange("p c t -> p (c t)"), bank(name),
                                 ACT.Copy).then_inc(s[done], 1)

        def biased_hi(name, n, dst, done):
            for c in range(KC):
                last = nc.scalar.activation(dst[:, c, :], bank(name)[:, c * TOK:(c + 1) * TOK],
                                            ACT.Identity, bias=bqk[:, n, c:c + 1])
            last.then_inc(s[done], 1)

        def exp(b, h):
            at_least(act, s["scoresT_filled"], b, HEADS, h + 1)
            at_least(act, s["pv_filled"], b if h >= 8 else b - 1, NQ, (h // QUAD - 2) % NQ + 1)
            nc.scalar.activation(probs[:, h % 8, :], st[:, h % 2, :], ACT.Exp).then_inc(s["exp_done"], 1)

        def save_quads(b, g):
            at_least(act, s["pv_filled"], b, NQ, g + 1)
            at_least(act, s["oT_filled"], b - 1, 2, 2)
            nc.scalar.activation(quad_sb[:, g - 1:g + 1, :], ov[:], ACT.Copy).then_inc(s["quad_saved"], 1)

        def m_to_row(b, g):
            at_least(act, s["mT_filled"], b, NQ, g + 1)
            at_least(act, m_placed[g % 2], b - 1, 16 * NQ // 2, 16 * NQ // 2)
            nc.scalar.activation(m_row[:, g, :], bank(f"m{g}")[0:QUAD, 0:TOK], ACT.Copy
                                 ).then_inc(s["m_row_done"], 1)

        def iteration(i, par):
            for step in range(HEADS):
                if step < EXP_LAG and active(i - 1):
                    exp(i - 1, step + HEADS - EXP_LAG)
                if step >= EXP_LAG and active(i):
                    exp(i, step - EXP_LAG)
                if PV_STEPS.get(step) in (1, 3) and active(i - 1):
                    save_quads(i - 1, PV_STEPS[step])
                if step == 2 and active(i - 1):
                    m_to_row(i - 1, 3)
                if step == 1 and active(i - 2):
                    at_least(act, s["attnT_filled"], i - 2, 1, 1)
                    at_least(act, s["proj_filled"], i - 3, 1, 1)
                    hi("attnT", attnT_hi, "attnT_hi_done")
                if step == 2 and active(i + 1):
                    at_least(act, s["ctx_in"], i + 1, 16, 16)
                    at_least(act, s["v_filled"], i, 1, 1)
                    nc.scalar.activation(ctxT_hi[:], ctxT[:], ACT.Copy).then_inc(s["ctxT_hi_done"], 1)
                if step == 6 and active(i + 1):
                    at_least(act, s["xT_filled"], i + 1, 1, 1)
                    at_least(act, s["q_filled"], i, 1, 1)
                    hi("xT", xT_hi, "xT_hi_done")
                if step == 8 and active(i + 1):
                    if at(i, -1):
                        act.wait_ge(s["bias_done"], 1)
                    at_least(act, s["k_filled"], i + 1, 1, 1)
                    at_least(act, s["k_stacked"], i, K_DMAS, K_DMAS)
                    biased_hi("k", 1, k_hi, "k_hi_done")
                if step == 5 and active(i):
                    m_to_row(i, 0)
                if step == 9 and active(i + 1):
                    at_least(act, s["q_filled"], i + 1, 1, 1)
                    at_least(act, s["q_stacked"], i, Q_DMAS, Q_DMAS)
                    biased_hi("q", 0, q_hi, "q_hi_done")
                if step == 9 and active(i):
                    m_to_row(i, 1)
                if step == 12 and active(i - 2):
                    at_least(act, s["xn2T_filled"], i - 2, 1, 1)
                    at_least(act, s["gate_filled"], i - 3, 1, 1)
                    nc.scalar.activation(xn2T[:].rearrange("p c t -> p (c t)"), bank("xn2T"),
                                         ACT.Copy).then_inc(s["xn2T_saved"], 1)
                if step == 14 and active(i):
                    m_to_row(i, 2)

        run(act, iteration)

    @block.vector
    def _(dve):
        def row_stats(rows, parts, mv, stats_done):
            for t in range(QT):
                last = nc.vector.bn_stats(parts[:, t, :], rows[:, t, :])
            dve.drain()
            for t in range(QT):
                last = nc.vector.bn_aggr(mv[:, t, :], parts[:, t, :])
            last.then_inc(s[stats_done], 1)

        def ln1_stats(b):
            at_least(dve, s["x_in"], b, 16, 16)
            at_least(dve, s["ln1_stats"], b - 1, 1, 1)
            at_least(dve, s["xn_done"], b - 1, 1, 1)
            row_stats(x_rows, stats1, mv1, "ln1_stats")

        ln1_stats(0)
        nc.vector.memset(ks[0][:].bitcast(F32), 0.0).then_inc(s["first_k_cleared"], 1)
        for p in range(2):
            nc.vector.memset(vals[p][:, :, :, HD:], 0.0).then_inc(s["values_cleared"], 1)
        dve.wait_ge(s["values_cleared"], 2)
        for p in range(2):
            nc.vector.memset(vals[p][:, :, :, HD], 1.0).then_inc(s["values_cleared"], 1)
        dve.wait_ge(s["weights_in"], WEIGHT_DMAS)
        nc.vector.tensor_scalar(bqk[:, 0], bqk[:, 0], 0.25, None, ALU.mult).then_inc(s["bias_done"], 1)
        for n in range(4):
            dve.wait_ge(s["w_hi_done"], n + 1)
            nc.vector.scalar_tensor_tensor(out=w_lo[:, n], in0=w_raw[:, n], scalar=0.25 if n == WQ else 1.0,
                                           in1=w_hi[:, n].bitcast(F32), op0=ALU.mult,
                                           op1=ALU.subtract).then_inc(s["w_lo_done"], 1)
        dve.wait_ge(s["bias_done"], 1)

        def row_max(i, par, h):
            at_least(dve, s["scores_filled"], i, HEADS, h + 1)
            if h % QUAD == 0:
                at_least(dve, s["mT_filled"], i - 1, NQ, h // QUAD + 1)
            nc.vector.tensor_reduce(neg_max[:, :, h:h + 1], mx[:, h % 2, :].rearrange("p (t k) -> p t k", t=QT),
                                    AX.X, ALU.max, negate=True).then_inc(s["max_done"], 1)

        def lo(name, dst_hi, dst_lo, done):
            nc.vector.tensor_tensor(dst_lo[:].rearrange("p c t -> p (c t)"), bank(name),
                                    dst_hi[:].rearrange("p c t -> p (c t)").bitcast(F32),
                                    ALU.subtract).then_inc(s[done], 1)

        def biased_lo(name, n, dst_hi, dst_lo, done):
            for c in range(KC):
                last = nc.vector.scalar_tensor_tensor(
                    out=dst_lo[:, c, :], in0=bank(name)[:, c * TOK:(c + 1) * TOK],
                    scalar=bqk[:, n, c:c + 1], in1=dst_hi[:, c, :].bitcast(F32),
                    op0=ALU.add, op1=ALU.subtract)
            last.then_inc(s[done], 1)

        def attention_rows(b, t):
            src = bank(f"oT{t}").rearrange("p (h e) -> p h e", e=32)
            at_least(dve, s["oT_filled"], b, 2, t + 1)
            at_least(dve, s["attn_done"], b - 1, 2, 2)
            nc.vector.reciprocal(recip[:, t, :].unsqueeze(2), src[:, :, HD:HD + 1]).then_inc(s["recip_done"], 1)
            at_least(dve, s["recip_done"], b, 2, t + 1)
            at_least(dve, s["attnT_filled"], b - 1, 1, 1)
            nc.vector.tensor_tensor(attn[:, t, :].rearrange("p (h e) -> p h e", e=HD), src[:, :, 0:HD],
                                    recip[:, t, :].unsqueeze(2).to_broadcast([P, HEADS, HD]),
                                    ALU.mult).then_inc(s["attn_done"], 1)

        def iteration(i, par):
            for step in range(HEADS):
                if active(i):
                    row_max(i, par, step)
                if step == 0 and active(i - 3):
                    at_least(dve, s["gate_filled"], i - 3, 1, 1)
                    nc.vector.tensor_copy(logits[:, bass.ds((i - 3) * (QT * EXPERTS), QT * EXPERTS)],
                                          bank("gate")[:, 0:QT * EXPERTS]).then_inc(s["gate_saved"], 1)
                if step == 2 and active(i - 2):
                    at_least(dve, s["proj_filled"], i - 3, 1, 1)
                    at_least(dve, s["attnT_hi_done"], i - 2, 1, 1)
                    lo("attnT", attnT_hi, attnT_lo, "attnT_lo_done")
                if step == 3 and active(i + 1):
                    at_least(dve, s["v_filled"], i, 1, 1)
                    at_least(dve, s["ctxT_hi_done"], i + 1, 1, 1)
                    nc.vector.tensor_tensor(ctxT_lo[:], ctxT[:], ctxT_hi[:].bitcast(F32),
                                            ALU.subtract).then_inc(s["ctxT_lo_done"], 1)
                if step == 4 and active(i - 2):
                    b = i - 2
                    at_least(dve, s["proj_filled"], b, 1, 1)
                    at_least(dve, s["x_res_done"], b, 1, 1)
                    at_least(dve, s["x2_stored"], b - 1, 16, 16)
                    at_least(dve, s["xn2_done"], b - 1, 1, 1)
                    nc.vector.tensor_tensor(x2[:].rearrange("p t d -> p (t d)"), bank("proj"),
                                            x_res[:].rearrange("p t d -> p (t d)"),
                                            ALU.add).then_inc(s["x2_done"], 1)
                if step == 5 and active(i - 2):
                    at_least(dve, s["x2_done"], i - 2, 1, 1)
                    at_least(dve, s["ln2_stats"], i - 3, 1, 1)
                    row_stats(x2, stats2, mv2, "ln2_stats")
                if step == 7 and active(i + 1):
                    at_least(dve, s["q_filled"], i, 1, 1)
                    at_least(dve, s["xT_hi_done"], i + 1, 1, 1)
                    lo("xT", xT_hi, xT_lo, "xT_lo_done")
                if step == 8 and active(i + 1):
                    at_least(dve, s["k_stacked"], i, K_DMAS, K_DMAS)
                    at_least(dve, s["k_hi_done"], i + 1, 1, 1)
                    biased_lo("k", 1, k_hi, k_lo, "k_lo_done")
                if step == 9 and active(i + 1):
                    at_least(dve, s["q_stacked"], i, Q_DMAS, Q_DMAS)
                    at_least(dve, s["q_hi_done"], i + 1, 1, 1)
                    biased_lo("q", 0, q_hi, q_lo, "q_lo_done")
                if step == 10 and active(i + 2):
                    ln1_stats(i + 2)
                if step == 12 and active(i + 1):
                    at_least(dve, s["v_filled"], i + 1, 1, 1)
                    at_least(dve, s["pv_filled"], i - 1, NQ, NQ)
                    nc.vector.tensor_tensor(
                        vals[(par + 1) % 2][:, :, :, 0:HD],
                        bank("v").rearrange("p (t h e) -> p t h e", t=QT, e=HD),
                        bv_all[:].rearrange("p (h e) -> p h e", e=HD).unsqueeze(1).to_broadcast([P, QT, HEADS, HD]),
                        ALU.add).then_inc(s["v_saved"], 1)
                if step in (13, 15) and active(i - 1):
                    attention_rows(i - 1, int(step == 15))

        run(dve, iteration)

    @block.gpsimd
    def _(pool):
        nc.gpsimd.memset(ones[:], 1.0)
        nc.gpsimd.memset(eps[:], EPS)
        nc.gpsimd.memset(zeros[:], 0.0).then_inc(s["ones_set"], 1)
        pool.drain()

        def normalise(rows, mv, tmp, dst, done):
            var, neg_mean, y, t = (tmp[:, n, :] for n in range(4))

            def then(_):
                pool.drain()

            then(nc.gpsimd.tensor_tensor(var, mv[:, :, 1], eps[:], ALU.add))
            then(nc.gpsimd.tensor_scalar(neg_mean, mv[:, :, 0], -1.0, None, ALU.mult))
            then(nc.gpsimd.tensor_scalar(y.bitcast(I32), var.bitcast(I32), -0.5, MAGIC, ALU.mult, ALU.add))
            for _ in range(NEWTON_STEPS):
                then(nc.gpsimd.tensor_tensor(t, y, y, ALU.mult))
                then(nc.gpsimd.tensor_tensor(t, t, var, ALU.mult))
                then(nc.gpsimd.tensor_scalar(t, t, -0.5, 1.5, ALU.mult, ALU.add))
                then(nc.gpsimd.tensor_tensor(y, y, t, ALU.mult))
            for t_ in range(QT):
                last = nc.gpsimd.tensor_scalar(dst[:, t_, :], rows[:, t_, :], neg_mean[:, t_:t_ + 1],
                                               y[:, t_:t_ + 1], ALU.add, ALU.mult)
            last.then_inc(s[done], 1)

        def first_norm(b):
            at_least(pool, s["ln1_stats"], b, 1, 1)
            at_least(pool, s["xn_done"], b - 1, 1, 1)
            at_least(pool, s["xT_filled"], b - 1, 1, 1)
            normalise(x_rows, mv1, norm1, xn, "xn_done")

        def iteration(i, par):
            if active(i - 2):
                b = i - 2
                at_least(pool, s["ln2_stats"], b, 1, 1)
                at_least(pool, s["xn2_done"], b - 1, 1, 1)
                at_least(pool, s["xn2T_filled"], b - 1, 1, 1)
                at_least(pool, s["xn2_stored"], b - 1, 16, 16)
                normalise(x2, mv2, norm2, xn2, "xn2_done")
            if active(i - 1):
                b = i - 1
                at_least(pool, s["x_again_in"], b, 16, 16)
                at_least(pool, s["x2_done"], b - 1, 1, 1)
                nc.gpsimd.tensor_tensor(x_res[:], x_again[:],
                                        bo_all[:].unsqueeze(1).to_broadcast([P, QT, D]),
                                        ALU.add).then_inc(s["x_res_done"], 1)
            if active(i + 2):
                first_norm(i + 2)

        first_norm(0)
        for rows in (qs[0], ks[1], qs[1]):
            nc.gpsimd.memset(rows[:].bitcast(F32), 0.0).then_inc(s["cleared"], 1)
        pool.wait_ge(s["weights_in"], WEIGHT_DMAS)
        run(pool, iteration)


def routing_program(nc, io, keep, ctx):
    def sb(name, shape, dt=F32):
        return ctx.enter_context(nc.sbuf_tensor(name, shape, dt))

    def sem(name):
        return ctx.enter_context(nc.semaphore(name))

    E, TE = EXPERTS, NT * EXPERTS
    PAIRS = 2 * NT
    RING = 3
    GROUP = 4
    later = sb("later", [P, P], BF16)
    later_f = sb("later_f", [P, P])
    ones = sb("ones_bf", [P, P], BF16)
    consts = sb("consts", [P, io["consts"].shape[1]])
    put = {name: consts[:, a:b] for name, (a, b) in CONST_COLS.items()}
    expl, score, masked, tmp = (sb(n, [P, NT, E]) for n in ("expl", "score", "masked", "tmp"))
    top1, top2, comb, rank = (sb(n, [P, NT, E]) for n in ("top1", "top2", "comb", "rank"))
    col = {n: sb("col_" + n, [P, NT]) for n in ("max", "sum", "inv", "v1", "v2", "f", "w1", "w2")}
    picks = sb("picks", [P, NT, E], BF16)
    picks_sum = sb("picks_sum", [P, E])
    picks_sum_bf = sb("picks_sum_bf", [P, E], BF16)
    count, tiles, before, until, base = (sb(n, [P, E]) for n in ("count", "tiles", "before", "until", "base"))
    passed = sb("passed", [P, E, NT])
    tri = sb("tri_tmp", [P, E, E])
    slot = sb("slot", [P, PAIRS])
    slot_i, tile_i, lane_i = (sb(n, [P, PAIRS], I32) for n in ("slot_i", "tile_i", "lane_i"))
    tile_f, lane_f = (sb(n, [P, PAIRS]) for n in ("tile_f", "lane_f"))
    lane_hot = sb("lane_hot", [P, RING, GROUP, P], F32R)
    tile_hot = sb("tile_hot", [P, RING, GROUP, SLOT_COLS])
    token_hot = sb("token_hot", [P, RING, GROUP, SLOT_COLS], F32R)
    slot_token, is_pad = (sb(n, [P, SLOT_COLS]) for n in ("slot_token", "is_pad"))
    owner = sb("owner", [P, SLOT_COLS, E - 1])
    gather_idx, scatter_idx, tile_expert = keep["gather_idx"], keep["scatter_idx"], keep["tile_expert"]
    w1_hi, w1_lo, w1_raw = keep["w1_hi"], keep["w1_lo"], keep["w1_raw"]
    wo_raw, wo_hi, wo_lo = sb("wo2_raw", [P, HID // P, D]), keep["wo_hi"], keep["wo_lo"]
    rank_ps = ctx.enter_context(nc.psum_tensor("rank_ps", [P, 512], F32))
    count_ps = ctx.enter_context(nc.psum_tensor("count_ps", [P, 512], F32))
    slot_ps = ctx.enter_context(nc.psum_tensor("slot_ps", [P, 512], F32))
    s = {n: sem("r_" + n) for n in (
        "consts_in wo_in b1_in w1_hi_done w1_lo_done wo_hi_done wo_lo_done dve_step "
        "exp_done picks_ready ones_ready counted ranked tile_hot_ready token_hot_ready hot_used slots_found comb_ready "
        "comb_stored max_taken").split()}
    w1_in = keep["w1_in"]
    logits = keep["logits"][:].rearrange("p (t e) -> p t e", e=E)
    block = ctx.enter_context(nc.Block())

    @block.sync
    def _(sp):
        sp.dma_start(consts[:], io["consts"]).then_inc(s["consts_in"], 16)
        sp.dma_start(later_f[:], io["later"]).then_inc(s["consts_in"], 16)
        for e in range(E // 2, E):
            sp.dma_start(w1_raw[:, :, e, :], expert_w1(io, e)).then_inc(w1_in[e], 16)
        sp.dma_start(wo_raw[:], io["WoT"].rearrange("(c p) n -> p c n", p=P)).then_inc(s["wo_in"], 16)
        sp.dma_start(keep["b1"][:], io["b1"].rearrange("e h -> (e h)").partition_broadcast(P)).then_inc(s["b1_in"], 16)
        sp.dma_start(keep["bo2"][:], io["bo2"].partition_broadcast(P)).then_inc(s["b1_in"], 16)
        sp.wait_ge(s["comb_ready"], 1)
        sp.dma_start(io["rows"][:, D:ROW].rearrange("(t p) e -> p t e", p=P), comb[:]).then_inc(s["comb_stored"], 16)
        sp.wait_ge(s["comb_stored"], 16)
        sp.wait_ge(s["b1_in"], 32)

    @block.scalar
    def _(act):
        act.wait_ge(s["max_taken"], 1)
        nc.scalar.activation(expl[:], masked[:], ACT.Exp).then_inc(s["exp_done"], 1)
        for e in range(E):
            act.wait_ge(w1_in[e], 16)
            nc.scalar.activation(w1_hi[:, :, e, :], w1_raw[:, :, e, :], ACT.Copy).then_inc(s["w1_hi_done"], 1)
        act.wait_ge(s["wo_in"], 16)
        nc.scalar.activation(wo_hi[:], wo_raw[:], ACT.Copy).then_inc(s["wo_hi_done"], 1)
        act.wait_ge(s["consts_in"], 32)
        for c in range(PAIRS):
            group, n = c // GROUP, c % GROUP
            act.wait_ge(s["tile_hot_ready"], group + 1)
            if group >= RING:
                act.wait_ge(s["hot_used"], c - RING * GROUP + 1)
            nc.scalar.activation(token_hot[:, group % RING, n, :], tile_hot[:, group % RING, n, :], ACT.Copy,
                                 scale=put["token"][:, c % NT:c % NT + 1]).then_inc(s["token_hot_ready"], 1)

    @block.gpsimd
    def _(pool):
        for e in range(E - 1):
            pool.wait_ge(s["w1_hi_done"], e + 1)
            nc.gpsimd.tensor_tensor(w1_lo[:, :, e, :], w1_raw[:, :, e, :], w1_hi[:, :, e, :].bitcast(F32),
                                    ALU.subtract).then_inc(s["w1_lo_done"], 1)
        pool.wait_ge(s["wo_hi_done"], 1)
        nc.gpsimd.tensor_tensor(wo_lo[:], wo_raw[:], wo_hi[:].bitcast(F32), ALU.subtract).then_inc(s["wo_lo_done"], 1)

    @block.tensor
    def _(pe):
        pe.wait_ge(s["ones_ready"], 1)
        pe.wait_ge(s["picks_ready"], 2)
        nc.tensor.matmul(count_ps[:, 0:E], ones[:], picks_sum_bf[:], start=True, stop=True).then_inc(s["counted"], 1)
        flat = picks[:].rearrange("p t e -> p (t e)")
        nc.tensor.matmul(rank_ps[:, 0:TE], later[:], flat, start=True, stop=False)
        for back in range(1, NT):
            last = nc.tensor.matmul(rank_ps[:, back * E:TE], ones[:], flat[:, 0:TE - back * E],
                                    start=False, stop=(back == NT - 1))
        last.then_inc(s["ranked"], 1)
        for c in range(PAIRS):
            group, n = c // GROUP, c % GROUP
            pe.wait_ge(s["token_hot_ready"], c + 1)
            nc.tensor.matmul(slot_ps[:, 0:SLOT_COLS], lane_hot[:, group % RING, n, :], token_hot[:, group % RING, n, :],
                             start=(c == 0), stop=(c == PAIRS - 1)).then_inc(s["hot_used"], 1)

    @block.vector
    def _(dve):
        steps = [0]

        def then(ins):
            steps[0] += 1
            ins.then_inc(s["dve_step"], 1)
            dve.wait_ge(s["dve_step"], steps[0])

        def by_token(column):
            return column.unsqueeze(2).to_broadcast([P, NT, E])

        tt, ts, red = nc.vector.tensor_tensor, nc.vector.tensor_scalar, nc.vector.tensor_reduce
        then(red(col["max"][:], logits, AX.X, ALU.max))
        tt(masked[:], logits, by_token(col["max"][:]), ALU.subtract).then_inc(s["max_taken"], 1)
        dve.wait_ge(s["exp_done"], 1)
        then(red(col["sum"][:], expl[:], AX.X, ALU.add))
        then(nc.vector.reciprocal(col["inv"][:], col["sum"][:]))
        then(tt(score[:], expl[:], by_token(col["inv"][:]), ALU.mult))
        dve.wait_ge(s["consts_in"], 32)
        then(nc.vector.tensor_copy(later[:], later_f[:]))
        nc.vector.memset(ones[:], 1.0).then_inc(s["ones_ready"], 1)

        def first_best(values, best, pick):
            then(red(best[:], values[:], AX.X, ALU.max))
            then(tt(tmp[:], values[:], by_token(best[:]), ALU.is_equal))
            then(tt(tmp[:], tmp[:], put["falling"].unsqueeze(1).to_broadcast([P, NT, E]), ALU.mult))
            then(red(col["f"][:], tmp[:], AX.X, ALU.max))
            then(tt(pick[:], tmp[:], by_token(col["f"][:]), ALU.is_equal))

        first_best(score, col["v1"], top1)
        then(nc.vector.scalar_tensor_tensor(out=masked[:], in0=top1[:], scalar=-2.0, in1=score[:],
                                            op0=ALU.mult, op1=ALU.add))
        first_best(masked, col["v2"], top2)
        then(tt(tmp[:], top1[:], top2[:], ALU.add))
        nc.vector.tensor_copy(picks[:], tmp[:]).then_inc(s["picks_ready"], 1)
        then(red(picks_sum[:], tmp[:].rearrange("p t e -> p e t"), AX.X, ALU.add))
        nc.vector.tensor_copy(picks_sum_bf[:], picks_sum[:]).then_inc(s["picks_ready"], 1)
        then(tt(col["sum"][:], col["v1"][:], col["v2"][:], ALU.add))
        then(ts(col["sum"][:], col["sum"][:], TOP_EPS, None, ALU.add))
        then(nc.vector.reciprocal(col["inv"][:], col["sum"][:]))
        then(tt(col["w1"][:], col["v1"][:], col["inv"][:], ALU.mult))
        then(tt(col["w2"][:], col["v2"][:], col["inv"][:], ALU.mult))
        then(tt(comb[:], top1[:], by_token(col["w1"][:]), ALU.mult))
        then(tt(masked[:], top2[:], by_token(col["w2"][:]), ALU.mult))
        tt(comb[:], comb[:], masked[:], ALU.add).then_inc(s["comb_ready"], 1)
        dve.wait_ge(s["counted"], 1)
        then(nc.vector.tensor_copy(count[:], count_ps[:, 0:E]))
        then(tt(passed[:], count[:].unsqueeze(2).to_broadcast([P, E, NT]),
                put["tile_starts"].unsqueeze(1).to_broadcast([P, E, NT]), ALU.is_gt))
        then(red(tiles[:], passed[:], AX.X, ALU.add))
        then(tt(tri[:], tiles[:].unsqueeze(1).to_broadcast([P, E, E]),
                put["below"].rearrange("p (a b) -> p a b", b=E), ALU.mult))
        then(red(before[:], tri[:], AX.X, ALU.add))
        then(tt(until[:], before[:], tiles[:], ALU.add))
        then(ts(base[:], before[:], float(P), None, ALU.mult))
        then(tt(owner[:], put["numbers"][:, 0:SLOT_COLS].unsqueeze(2).to_broadcast([P, SLOT_COLS, E - 1]),
                until[:, 0:E - 1].unsqueeze(1).to_broadcast([P, SLOT_COLS, E - 1]), ALU.is_ge))
        then(red(slot_token[:], owner[:], AX.X, ALU.add))
        then(nc.vector.tensor_copy(tile_expert[:], slot_token[:]))
        dve.wait_ge(s["ranked"], 1)
        then(tt(rank[:], rank_ps[:, 0:TE].rearrange("p (t e) -> p t e", e=E),
                base[:].unsqueeze(1).to_broadcast([P, NT, E]), ALU.add))
        for n, top in enumerate((top1, top2)):
            then(tt(tmp[:], top[:], rank[:], ALU.mult))
            then(red(slot[:, n * NT:(n + 1) * NT], tmp[:], AX.X, ALU.add))
        then(nc.vector.tensor_copy(slot_i[:], slot[:]))
        then(ts(tile_i[:], slot_i[:], 7, None, ALU.arith_shift_right))
        then(ts(lane_i[:], slot_i[:], P - 1, None, ALU.bitwise_and))
        then(nc.vector.tensor_copy(tile_f[:], tile_i[:]))
        then(nc.vector.tensor_copy(lane_f[:], lane_i[:]))
        for group in range(PAIRS // GROUP):
            if group >= RING:
                dve.wait_ge(s["hot_used"], (group - RING + 1) * GROUP)
            cols = slice(group * GROUP, (group + 1) * GROUP)
            tt(lane_hot[:, group % RING], put["numbers"].unsqueeze(1).to_broadcast([P, GROUP, P]),
               lane_f[:, cols].unsqueeze(2).to_broadcast([P, GROUP, P]), ALU.is_equal)
            tt(tile_hot[:, group % RING], put["numbers"][:, 0:SLOT_COLS].unsqueeze(1).to_broadcast([P, GROUP, SLOT_COLS]),
               tile_f[:, cols].unsqueeze(2).to_broadcast([P, GROUP, SLOT_COLS]), ALU.is_equal
               ).then_inc(s["tile_hot_ready"], 1)
        dve.wait_ge(s["w1_hi_done"], E)
        tt(w1_lo[:, :, E - 1, :], w1_raw[:, :, E - 1, :], w1_hi[:, :, E - 1, :].bitcast(F32), ALU.subtract
           ).then_inc(s["w1_lo_done"], 1)
        dve.wait_ge(s["hot_used"], PAIRS)
        then(nc.vector.tensor_copy(slot_token[:], slot_ps[:, 0:SLOT_COLS]))
        then(ts(is_pad[:], slot_token[:], 0.0, None, ALU.is_equal))
        then(ts(is_pad[:], is_pad[:], put["spare_row"], None, ALU.mult))
        then(ts(slot_token[:], slot_token[:], -1.0, None, ALU.add))
        then(tt(is_pad[:], is_pad[:], slot_token[:], ALU.add))
        then(nc.vector.tensor_copy(scatter_idx[:], is_pad[:]))
        then(ts(slot_token[:], slot_token[:], 0.0, None, ALU.max))
        then(nc.vector.tensor_copy(gather_idx[:], slot_token[:]))


SLOT_COLS = SLOT_TILES + SLOT_TILES % 2
CONST_COLS, _at = {}, 0
for _name, _n in (("falling", EXPERTS), ("below", EXPERTS * EXPERTS), ("tile_starts", NT),
                  ("numbers", P), ("token", NT), ("spare_row", 1)):
    CONST_COLS[_name] = (_at, _at + _n)
    _at += _n


def constants():
    one = np.ones((P, 1), np.float32)
    lane = np.arange(P, dtype=np.float32)[:, None]
    e = np.arange(EXPERTS)
    return np.concatenate([
        one * (EXPERTS - e),
        one * (e[None, :] < e[:, None]).reshape(1, -1),
        one * (P * np.arange(NT)),
        one * np.arange(P),
        lane + P * np.arange(NT) + 1,
        lane + TOKENS + 1,
    ], axis=1).astype(np.float32)


def expert_program(nc, io, keep, ctx):
    def sb(name, shape, dt=F32):
        return ctx.enter_context(nc.sbuf_tensor(name, shape, dt))

    def sem(name):
        return ctx.enter_context(nc.semaphore(name))

    HC = HID // P
    ident, w1_hi, w1_lo, wo_hi, wo_lo = (keep[n] for n in ("ident", "w1_hi", "w1_lo", "wo_hi", "wo_lo"))
    b1, bo2, tile_expert = keep["b1"], keep["bo2"], keep["tile_expert"]
    rows = [sb(f"rows{p}", [P, ROW]) for p in range(2)]
    from_rows = [sb(f"from_rows{p}", [P, 1], U32) for p in range(2)]
    to_rows = [sb(f"to_rows{p}", [P, 1], U32) for p in range(2)]
    weight = sb("weight", [P, SLOT_COLS])
    xT_hi = [sb(f"xT_hi{p}", [P, KC, P], F32R) for p in range(2)]
    xT_lo = [sb(f"xT_lo{p}", [P, KC, P], F32R) for p in range(2)]
    gate_in, sig, up = sb("gate_in", [P, HID]), sb("sig", [P, HID]), sb("up", [P, HID])
    g = sb("g", [P, HID])
    gT_hi, gT_lo = sb("gT_hi", [P, HC, P], F32R), sb("gT_lo", [P, HC, P], F32R)
    y_biased = sb("y_biased", [P, D])
    y = [sb(f"y{p}", [P, D]) for p in range(2)]
    hb_ps = ctx.enter_context(nc.psum_tensor("hb_ps", [P, 2, 512], F32))
    ha_ps = ctx.enter_context(nc.psum_tensor("ha_ps", [P, 2, 512], F32))
    y_ps = ctx.enter_context(nc.psum_tensor("y_ps", [P, 2, 512], F32))
    xT_ps = ctx.enter_context(nc.psum_tensor("xT_ps", [P, 512], F32))
    gT_ps = ctx.enter_context(nc.psum_tensor("gT_ps", [P, 512], F32))
    s = {n: sem("e_" + n) for n in (
        "xT_filled xT_hi_done xT_lo_done weight_saved hb_filled ha_filled gate_in_done "
        "sig_done up_done g_done gT_filled gT_hi_done gT_lo_done y_filled y_biased_done y_done "
        "gathers_begun scatters_begun from_rows_set to_rows_set scattered").split()}

    def active(t, lag):
        return not isinstance(t, int) or 0 <= t + lag < SLOT_TILES

    def past(eng, sem_, t):
        at_least(eng, sem_, t, 1, 1)

    def run(eng, iteration):
        for t in range(-1, 4):
            iteration(t, t % 2)
        with eng.Fori(2, (SLOT_TILES - 3) // 2) as pair:
            iteration(pair * 2, 0)
            iteration(pair * 2 + 1, 1)
        for t in range((SLOT_TILES - 3) // 2 * 2, SLOT_TILES + 2):
            iteration(t, t % 2)

    gathered = [sem(f"e_gathered{p}") for p in range(2)]

    def rows_there(eng, t, par):
        at_least(eng, gathered[par], t - par, 8, 16)

    def expert_of(eng, t):
        return eng.value_load(tile_expert[0:1, bass.ds(t, 1)], min_val=0, max_val=EXPERTS - 1)

    block = ctx.enter_context(nc.Block())

    @block.gpsimd
    def _(pool):
        def gather(t, par):
            past(pool, s["xT_filled"], t - 2)
            past(pool, s["weight_saved"], t - 2)
            rows_there(pool, t - 2, par)
            nc.gpsimd.tensor_copy(from_rows[par][:], keep["gather_idx"][:, bass.ds(t, 1)]
                                  ).then_inc(s["from_rows_set"], 1)
            past(pool, s["from_rows_set"], t)
            pool.sem_inc(s["gathers_begun"], 1)
            nc.gpsimd.indirect_dma_start(
                out=rows[par][:], out_offset=None, in_=io["rows"],
                in_offset=bass.IndirectOffsetOnAxis(ap=from_rows[par][:], axis=0)
            ).then_inc(gathered[par], 16)

        def iteration(t, par):
            if active(t, 2):
                gather(t + 2, par)
            if active(t, -2):
                at_least(pool, s["scattered"], t - 4, 16, 16)
                nc.gpsimd.tensor_copy(to_rows[par][:], keep["scatter_idx"][:, bass.ds(t - 2, 1)]
                                      ).then_inc(s["to_rows_set"], 1)
                past(pool, s["to_rows_set"], t - 2)
                past(pool, s["y_done"], t - 2)
                at_least(pool, s["scattered"], t - 3, 16, 16)
                pool.sem_inc(s["scatters_begun"], 1)
                nc.gpsimd.indirect_dma_start(
                    out=io["out"], in_=y[par][:], in_offset=None, compute_op=ALU.add,
                    out_offset=bass.IndirectOffsetOnAxis(ap=to_rows[par][:], axis=0)
                ).then_inc(s["scattered"], 16)

        gather(0, 0)
        run(pool, iteration)
        pool.wait_ge(s["scattered"], 16 * SLOT_TILES)

    @block.tensor
    def _(pe):
        def first_product(t, par, e, half, out, filled):
            first = True
            for c in range(KC):
                cols = bass.ds(e * (2 * HID) + half * HID, HID)
                w_hi, w_lo = (w[:, c].rearrange("p e h -> p (e h)")[:, cols] for w in (w1_hi, w1_lo))
                nc.tensor.matmul(out, xT_hi[par][:, c, :], w_hi, start=first, stop=False)
                nc.tensor.matmul(out, xT_hi[par][:, c, :], w_lo, start=False, stop=False)
                last = nc.tensor.matmul(out, xT_lo[par][:, c, :], w_hi, start=False, stop=(c == KC - 1))
                first = False
            last.then_inc(s[filled], 1)

        def iteration(t, par):
            other = (par + 1) % 2
            if active(t, 0):
                e = expert_of(pe, t)
            if active(t, -2):
                past(pe, s["gT_hi_done"], t - 2)
                past(pe, s["y_biased_done"], t - 4)
                out = y_ps[:, par, 0:D]
                for c in range(HC):
                    nc.tensor.matmul(out, gT_hi[:, c, :], wo_hi[:, c, :], start=(c == 0), stop=False)
                    nc.tensor.matmul(out, gT_hi[:, c, :], wo_lo[:, c, :], start=False, stop=False)
                past(pe, s["gT_lo_done"], t - 2)
                for c in range(HC):
                    last = nc.tensor.matmul(out, gT_lo[:, c, :], wo_hi[:, c, :], start=False, stop=(c == HC - 1))
                last.then_inc(s["y_filled"], 1)
            if active(t, 0):
                past(pe, s["xT_lo_done"], t)
                past(pe, s["gate_in_done"], t - 2)
                first_product(t, par, e, 1, hb_ps[:, par, :], "hb_filled")
            if active(t, -1):
                past(pe, s["g_done"], t - 1)
                past(pe, s["gT_lo_done"], t - 2)
                for c in range(HC):
                    last = nc.tensor.transpose(gT_ps[:, c * P:(c + 1) * P], g[:, c * P:(c + 1) * P], ident[:])
                last.then_inc(s["gT_filled"], 1)
            if active(t, 1):
                rows_there(pe, t + 1, other)
                past(pe, s["xT_lo_done"], t)
                for c in range(KC):
                    last = nc.tensor.transpose(xT_ps[:, c * P:(c + 1) * P],
                                               rows[other][:, c * P:(c + 1) * P], ident[:])
                last.then_inc(s["xT_filled"], 1)
            if active(t, 0):
                past(pe, s["up_done"], t - 2)
                first_product(t, par, e, 0, ha_ps[:, par, :], "ha_filled")

        run(pe, iteration)

    @block.scalar
    def _(act):
        def iteration(t, par):
            other = (par + 1) % 2
            if active(t, -2):
                past(act, s["y_biased_done"], t - 2)
                at_least(act, s["scattered"], t - 4, 16, 16)
                nc.scalar.activation(y[par][:], y_biased[:], ACT.Copy,
                                     scale=weight[:, bass.ds(t - 2, 1)]).then_inc(s["y_done"], 1)
            if active(t, -1):
                past(act, s["gT_filled"], t - 1)
                past(act, s["y_filled"], t - 2)
                nc.scalar.activation(gT_hi[:].rearrange("p c t -> p (c t)"), gT_ps[:], ACT.Copy
                                     ).then_inc(s["gT_hi_done"], 1)
            if active(t, 1):
                past(act, s["xT_filled"], t + 1)
                past(act, s["ha_filled"], t - 1)
                nc.scalar.activation(xT_hi[other][:].rearrange("p c t -> p (c t)"), xT_ps[:, 0:KC * P],
                                     ACT.Copy).then_inc(s["xT_hi_done"], 1)
            if active(t, 0):
                past(act, s["gate_in_done"], t)
                past(act, s["g_done"], t - 1)
                nc.scalar.activation(sig[:], gate_in[:], ACT.Sigmoid).then_inc(s["sig_done"], 1)

        run(act, iteration)

    @block.vector
    def _(dve):
        def iteration(t, par):
            other = (par + 1) % 2
            if active(t, -2):
                past(dve, s["y_filled"], t - 2)
                past(dve, s["y_done"], t - 3)
                nc.vector.tensor_tensor(y_biased[:], y_ps[:, par, 0:D], bo2[:], ALU.add
                                        ).then_inc(s["y_biased_done"], 1)
            if active(t, 0):
                e = expert_of(dve, t)
            if active(t, 1):
                e_next = expert_of(dve, t + 1)
            if active(t, 0):
                past(dve, s["hb_filled"], t)
                past(dve, s["sig_done"], t - 1)
                nc.vector.tensor_tensor(gate_in[:], hb_ps[:, par, :], b1[:, bass.ds(e * (2 * HID) + HID, HID)],
                                        ALU.add).then_inc(s["gate_in_done"], 1)
            if active(t, -1):
                past(dve, s["gT_hi_done"], t - 1)
                past(dve, s["y_filled"], t - 2)
                nc.vector.tensor_tensor(gT_lo[:].rearrange("p c t -> p (c t)"), gT_ps[:],
                                        gT_hi[:].rearrange("p c t -> p (c t)").bitcast(F32),
                                        ALU.subtract).then_inc(s["gT_lo_done"], 1)
            if active(t, 1):
                rows_there(dve, t + 1, other)
                nc.vector.tensor_copy(weight[:, bass.ds(t + 1, 1)], rows[other][:, bass.ds(e_next + D, 1)]
                                      ).then_inc(s["weight_saved"], 1)
                past(dve, s["xT_hi_done"], t + 1)
                past(dve, s["ha_filled"], t - 1)
                nc.vector.tensor_tensor(xT_lo[other][:].rearrange("p c t -> p (c t)"), xT_ps[:, 0:KC * P],
                                        xT_hi[other][:].rearrange("p c t -> p (c t)").bitcast(F32),
                                        ALU.subtract).then_inc(s["xT_lo_done"], 1)
            if active(t, 0):
                past(dve, s["ha_filled"], t)
                past(dve, s["g_done"], t - 1)
                nc.vector.tensor_tensor(up[:], ha_ps[:, par, :], b1[:, bass.ds(e * (2 * HID), HID)],
                                        ALU.add).then_inc(s["up_done"], 1)
                past(dve, s["up_done"], t)
                past(dve, s["sig_done"], t)
                past(dve, s["gT_filled"], t - 1)
                nc.vector.tensor_tensor(g[:], up[:], sig[:], ALU.mult).then_inc(s["g_done"], 1)

        run(dve, iteration)


def build(nc, io, phases=3):
    with ExitStack() as ctx:
        keep = {"ident": ctx.enter_context(nc.sbuf_tensor("ident", [P, P], F32)),
                "logits": ctx.enter_context(nc.sbuf_tensor("logits", [P, NT * EXPERTS], F32))}
        with nc.sbuf_tensor("w1_raw", [P, KC, EXPERTS, 2 * HID], F32) as w1_raw:
            keep["w1_raw"] = w1_raw
        keep["w1_in"] = [ctx.enter_context(nc.semaphore(f"w1_in{e}")) for e in range(EXPERTS)]
        with ExitStack() as stage:
            attention_program(nc, io, keep, stage)
        if phases >= 2:
            hold = lambda name, shape, dt=F32: ctx.enter_context(nc.sbuf_tensor(name, shape, dt))
            keep["w1_lo"] = hold("w1_lo", [P, KC, EXPERTS, 2 * HID], F32R)
            keep["w1_hi"] = hold("w1_hi", [P, KC, EXPERTS, 2 * HID], F32R)
            keep["wo_hi"] = hold("wo2_hi", [P, HID // P, D], F32R)
            keep["wo_lo"] = hold("wo2_lo", [P, HID // P, D], F32R)
            keep["b1"] = hold("b1_all", [P, EXPERTS * 2 * HID])
            keep["bo2"] = hold("bo2_all", [P, D])
            keep["gather_idx"] = hold("gather_idx", [P, SLOT_COLS], U32)
            keep["scatter_idx"] = hold("scatter_idx", [P, SLOT_COLS], U32)
            keep["tile_expert"] = hold("tile_expert", [P, SLOT_COLS], I32)
            with ExitStack() as stage:
                routing_program(nc, io, keep, stage)
            if phases == 3:
                with ExitStack() as stage:
                    expert_program(nc, io, keep, stage)
        if phases == 1:
            dsem = ctx.enter_context(nc.semaphore("dbg"))
            with nc.Block() as block:
                @block.sync
                def _(sp):
                    sp.dma_start(io["dbg"], keep["logits"][:]).then_inc(dsem, 16)
                    sp.wait_ge(dsem, 16)


def layouts(inputs):
    g = {k: np.asarray(v) for k, v in inputs.items()}
    heads_last = np.arange(D).reshape(HEADS // KC, KC, HD).transpose(1, 2, 0).reshape(-1)
    for n in ("Wq", "Wk", "bq", "bk"):
        g["L0_xattn_" + n] = np.ascontiguousarray(g["L0_xattn_" + n][..., heads_last])
    return {
        "x": g["x"], "ctxT": np.ascontiguousarray(g["ctx_1024"].transpose(0, 2, 1)),
        "Wq": g["L0_xattn_Wq"], "Wk": g["L0_xattn_Wk"], "Wv": g["L0_xattn_Wv"], "Wo": g["L0_xattn_Wo"],
        "bq": g["L0_xattn_bq"], "bk": g["L0_xattn_bk"], "bv": g["L0_xattn_bv"], "bo": g["L0_xattn_bo"],
        "WgT": np.ascontiguousarray(g["L0_ffn_Wg"].T),
        "W1T": np.ascontiguousarray(g["L0_ffn_W1"].transpose(2, 0, 1)),
        "b1": g["L0_ffn_b1"], "WoT": np.ascontiguousarray(g["L0_ffn_Wo"].T), "bo2": g["L0_ffn_bo"],
        "ident": np.eye(P, dtype=np.float32),
        "later": np.triu(np.ones((P, P), np.float32), 1),
        "consts": constants(),
    }


def kernel(**inputs):
    import concourse.bacc as bacc
    from concourse.bass_utils import run_bass_kernel_spmd

    arrays = {f"in_{name}": a for name, a in layouts(inputs).items()}
    nc = bacc.Bacc("TRN2", target_bir_lowering=False, num_devices=1)
    io = {name[3:]: nc.dram_tensor(name, a.shape, mybir.dt.from_np(a.dtype), kind="ExternalInput").ap()
          for name, a in arrays.items()}
    io["out"] = nc.dram_tensor("out_rows", (TOKENS + P, D), F32, kind="ExternalOutput").ap()
    io["rows"] = nc.dram_tensor("token_rows", (TOKENS, ROW), F32, kind="Internal").ap()
    build(nc, io)
    r = run_bass_kernel_spmd(nc, [arrays], core_ids=[0])
    return r.results[0]["out_rows"][0:TOKENS].reshape(BATCH, TOK, D)
```
